# Optimizing a Trainium2 kernel written in Bass

```python
import numpy as np
import jax
import jax.numpy as jnp

def _softmax(x, axis=-1):
    return jax.nn.softmax(x, axis=axis)

def _gelu(x):
    return jax.nn.gelu(x, approximate=True)

def _silu(x):
    return jax.nn.silu(x)

def _sigmoid(x):
    return jax.nn.sigmoid(x)

def _layernorm(x, axis=-1, eps=1e-05):
    m = jnp.mean(x, axis=axis, keepdims=True)
    v = jnp.var(x, axis=axis, keepdims=True)
    return (x - m) / jnp.sqrt(v + eps)

def _scatter_add(tgt, idx, src, axis=0):
    return tgt.at[idx].add(src)

def _segment_sum(src, seg, n):
    return jax.ops.segment_sum(src, seg, n)
kernel_name = 'mk_xattn_ffn_d1_seqx_r8_7915dc'

def setup_inputs(seed: int=0):
    np.random.seed(seed)
    _w = jnp.asarray

    def _rec_inputs():
        import jax
        import jax.numpy as jnp
        _rk = jax.random.key(seed)
        x = 7.22e-05 + 1 * jax.random.normal(jax.random.fold_in(_rk, 1), (8, 128, 256), jnp.float32)
        _lenS = 128 - jax.random.randint(jax.random.fold_in(_rk, 7), (8,), 0, max(1, 128 // 4) + 1, jnp.int32)
        _lenS2 = 128 - jax.random.randint(jax.random.fold_in(_rk, 8), (8,), 0, max(1, 128 // 4) + 1, jnp.int32)
        _ctx_2048P = jax.random.normal(jax.random.fold_in(_rk, 11), (8, 16, 256), jnp.float32)
        _ctx_2048c = jax.random.dirichlet(jax.random.fold_in(_rk, 511), 0.3 * jnp.ones((16,), jnp.float32), (8, 128))
        _ctx_2048t = jnp.einsum('bsk,bkd->bsd', _ctx_2048c, _ctx_2048P)
        _ctx_2048t = _ctx_2048t * jax.lax.rsqrt(jnp.mean(jnp.square(_ctx_2048t)) + 1e-12) * 0.953939
        ctx_2048 = 4.13588e-05 + 0.999923 * (_ctx_2048t + 0.3 * jax.random.normal(jax.random.fold_in(_rk, 611), (8, 128, 256), jnp.float32))
        return (x, ctx_2048)
    x, ctx_2048 = _rec_inputs()

    def _L0_xattn_setup():
        import jax, jax.numpy as jnp
        import numpy as np
        N_HEAD = 8
        key = jax.random.key(seed)
        k1, k2, k3 = jax.random.split(key, 3)
        b, d, m = (4, 128, 256)
        c, n = (128, 256)
        q = jax.random.normal(k1, (b, d, m), dtype=jnp.float32)
        k = jax.random.normal(k2, (d // d * b, d, n), dtype=jnp.float32).reshape(b, d, n)
        v = jax.random.normal(k3, (b, c, n), dtype=jnp.float32)
        return {'q': q, 'k': k, 'v': v}
    _L0_xattn_all = _L0_xattn_setup()
    _L0_xattn_in = {k: v for k, v in _L0_xattn_all.items() if k in ()}
    del _L0_xattn_all

    def _L0_ffn_setup():
        import jax, jax.numpy as jnp
        import numpy as np
        B, S, D = (4, 256, 256)
        DFF = 704
        E, K, R = (8, 2, 16)
        SCALING = 32.0 / 16.0
        key = jax.random.key(seed)
        ks = jax.random.split(key, 12)
        s = lambda k, shape, scale: jax.random.normal(k, shape, dtype=jnp.float32) * scale
        return {'x': s(ks[0], (B, S, D), 1.0), 'Wg': s(ks[1], (DFF, D), 0.02), 'Wu': s(ks[2], (DFF, D), 0.02), 'Wd': s(ks[3], (D, DFF), 0.02), 'Wr': s(ks[4], (E, D), 0.02), 'Ag': s(ks[5], (E, R, D), 0.02), 'Bg': s(ks[6], (E, DFF, R), 0.02), 'Au': s(ks[7], (E, R, D), 0.02), 'Bu': s(ks[8], (E, DFF, R), 0.02), 'Ad': s(ks[9], (E, R, DFF), 0.02), 'Bd': s(ks[10], (E, D, R), 0.02)}
    _L0_ffn_all = _L0_ffn_setup()
    _L0_ffn_in = {k: v for k, v in _L0_ffn_all.items() if k in ('Wg', 'Wu', 'Wd', 'Wr', 'Ag', 'Bg', 'Au', 'Bu', 'Ad', 'Bd')}
    del _L0_ffn_all
    return {'x': x, 'ctx_2048': ctx_2048, 'L0_ffn_Wg': _L0_ffn_in['Wg'], 'L0_ffn_Wu': _L0_ffn_in['Wu'], 'L0_ffn_Wd': _L0_ffn_in['Wd'], 'L0_ffn_Wr': _L0_ffn_in['Wr'], 'L0_ffn_Ag': _L0_ffn_in['Ag'], 'L0_ffn_Bg': _L0_ffn_in['Bg'], 'L0_ffn_Au': _L0_ffn_in['Au'], 'L0_ffn_Bu': _L0_ffn_in['Bu'], 'L0_ffn_Ad': _L0_ffn_in['Ad'], 'L0_ffn_Bd': _L0_ffn_in['Bd']}

def reference(x, ctx_2048, L0_ffn_Wg, L0_ffn_Wu, L0_ffn_Wd, L0_ffn_Wr, L0_ffn_Ag, L0_ffn_Bg, L0_ffn_Au, L0_ffn_Bu, L0_ffn_Ad, L0_ffn_Bd):
    import jax
    import jax.numpy as jnp

    def _L0_xattn_ref(q, k, v):
        import jax, jax.numpy as jnp
        import numpy as np
        N_HEAD = 8
        b, d, m = q.shape
        c = v.shape[1]
        h = N_HEAD
        qh = q.reshape(b * h, d // h, m)
        kh = k.reshape(b * h, d // h, -1)
        vh = v.reshape(b * h, c // h, -1)
        scale = 1.0 / jnp.sqrt(jnp.asarray(d // h, dtype=q.dtype))
        qk = jnp.einsum('bdm,bdn->bmn', qh, kh) * scale
        sm = jax.nn.softmax(qk, axis=-1)
        ret = jnp.einsum('bmn,bcn->bcm', sm, vh)
        return ret.reshape(b, c, m)

    def _L0_ffn_ref(x, Wg, Wu, Wd, Wr, Ag, Bg, Au, Bu, Ad, Bd):
        import jax, jax.numpy as jnp
        import numpy as np
        B, S, D = (4, 256, 256)
        DFF = 704
        E, K, R = (8, 2, 16)
        SCALING = 32.0 / 16.0
        b, s, d = x.shape
        xf = x.reshape(-1, d)
        gate_base = xf @ Wg.T
        up_base = xf @ Wu.T
        base_out = jax.nn.silu(gate_base) * up_base @ Wd.T
        router_logits = xf @ Wr.T
        probs = jax.nn.softmax(router_logits.astype(jnp.float32), axis=-1)
        topw, topi = jax.lax.top_k(probs, K)
        topw = topw.astype(x.dtype)
        expert_w = jnp.sum(jax.nn.one_hot(topi, E, dtype=x.dtype) * topw[..., None], axis=1)

        def expert_step(acc, params):
            Ag_e, Bg_e, Au_e, Bu_e, Ad_e, Bd_e, we = params
            g_lora = xf @ Ag_e.T @ Bg_e.T * SCALING
            u_lora = xf @ Au_e.T @ Bu_e.T * SCALING
            h = jax.nn.silu(gate_base + g_lora) * (up_base + u_lora)
            d_delta = h @ Ad_e.T @ Bd_e.T * SCALING
            return (acc + d_delta * we[:, None], None)
        acc0 = jnp.zeros_like(base_out)
        acc, _ = jax.lax.scan(expert_step, acc0, (Ag, Bg, Au, Bu, Ad, Bd, expert_w.T))
        return (base_out + acc).reshape(b, s, d)
    x = x + _L0_xattn_ref(_layernorm(x, axis=-1), ctx_2048, ctx_2048)
    x = x + _L0_ffn_ref(_layernorm(x, axis=-1), L0_ffn_Wg, L0_ffn_Wu, L0_ffn_Wd, L0_ffn_Wr, L0_ffn_Ag, L0_ffn_Bg, L0_ffn_Au, L0_ffn_Bu, L0_ffn_Ad, L0_ffn_Bd)
    return x

_drawn_inputs = setup_inputs


def setup_inputs(seed=0):
    import zlib

    import numpy as np

    out = dict(_drawn_inputs(seed))
    spreads = {}
    factors = {'L0_ffn_Wr': 8.0,
     'L0_ffn_Ag': 8.0,
     'L0_ffn_Bg': 8.0,
     'L0_ffn_Au': 8.0,
     'L0_ffn_Bu': 8.0,
     'L0_ffn_Ad': 8.0,
     'L0_ffn_Bd': 8.0,
     'L0_ffn_Wd': 41.618}
    for name, (base, spread) in spreads.items():
        noise = np.random.default_rng([zlib.crc32(name.encode()), seed]).standard_normal(out[name].shape)
        drawn = base * np.exp(spread * noise) if base else spread * noise
        out[name] = jnp.asarray(drawn.astype(out[name].dtype))
    for name, factor in factors.items():
        out[name] = (out[name] * factor).astype(out[name].dtype)
    return out
```

```python
from contextlib import ExitStack

import concourse.bass as bass
from concourse import mybir

F32 = mybir.dt.float32
F32R = mybir.dt.float32r
I32 = mybir.dt.int32
U32 = mybir.dt.uint32
ALU = mybir.AluOpType
ACT = mybir.ActivationFunctionType
AX = mybir.AxisListType

B, R, D = 8, 128, 256
H, HD = 8, 16
SCALE = float(HD) ** -0.5
F = 704
E, RANK = 8, 16
LORA = 2.0
EPS = 1e-5
NT = B * R
KD = D // 128
MT = (F + 127) // 128
TAIL = F - (MT - 1) * 128
C = 512
NC = NT // C
TC = C // 128
ORDER = [0, 2, 4, 6, 1, 3, 5, 7]
NQ = 3
MAXROW = 96
RSQRT_SEED = 0x5F3759DF

PIECES = [("wg", KD * MT * 128), ("wu", KD * (MT - 1) * 128), ("ag", KD * 128), ("au", KD * 128),
          ("wr", KD * E), ("bg", MT * 128), ("bu", MT * 128), ("wd", MT * D), ("ad", MT * 128), ("bd", D)]
AT = {}
NW = 0
for _name, _n in PIECES:
    AT[_name] = NW
    NW += _n
WPARTS = 10
WP = NW // WPARTS


def xattn_lora_ffn_kernel(nc, x, ctx_in, ctxT, weights, sel, out):
    xv = x.rearrange("b r d -> r b d")
    cv = ctx_in.rearrange("b r d -> r b d")
    tv = ctxT.rearrange("b (k p) r -> p b k r", p=128)
    ov = out.rearrange("b r d -> r b d")
    scratch = nc.dram_tensor("scratch", [B, 4, R, D], F32, kind="Internal").ap()

    with ExitStack() as ctx:
        def sb(name, shape, dt=F32, to=None):
            return (to or ctx).enter_context(nc.sbuf_tensor(name, shape, dt))

        def sem(name):
            return ctx.enter_context(nc.semaphore(name))

        bank = [ctx.enter_context(nc.psum_tensor(f"bank{i}", [128, 512], F32)) for i in range(8)]
        S_BANK, ST_BANK, MAX_BANK, U_BANK, Z_BANK = bank[0:2], bank[2:4], bank[4], bank[5], bank[6]
        GU_BANK, O_BANK, D_BANK = [bank[0:2], bank[2:4]], bank[4:6], bank[6:8]

        x_sb = sb("x_sb", [128, B, D])
        x1 = sb("x1", [128, B, D])
        w_hi = sb("w_hi", [128, NW], F32R)
        w_lo = sb("w_lo", [128, NW], F32R)
        w_raw = sb("w_raw", [128, 2, WP])
        ident = sb("ident", [128, 128])
        stats = sb("stats", [128, 2, B, 6])
        mv = sb("mv", [128, 2, B, 2])
        rstd = sb("rstd", [128, 2, B])
        nr_v = sb("nr_v", [128, B])
        nr_t = sb("nr_t", [128, B])
        xT_hi = sb("xT_hi", [128, KD, NT], F32R)
        xT_lo = sb("xT_lo", [128, KD, NT], F32R)
        xn2 = sb("xn2", [128, 2, D])

        att = ExitStack()
        c_sb = sb("c_sb", [128, B, D], to=att)
        ct_sb = sb("ct_sb", [128, B, 2, R], to=att)
        qf = sb("qf", [128, 2, D], to=att)
        split = sb("split", [128, 2, 4, D], F32R, to=att)
        Q = sb("Q", [128, NQ, H, D], F32R, to=att)
        K = sb("K", [128, NQ, H, D], F32R, to=att)
        sel_sb = sb("sel_sb", [128, H, D], to=att)
        V = sb("V", [128, 2, 2, H, 32], to=att)
        ones = sb("ones", [128, 2, 32], to=att)
        P = sb("P", [128, H, 2, D], to=att)
        mx = sb("mx", [128, 2, 2, H], to=att)
        mx_split = sb("mx_split", [128, 2, 2, 2, H], F32R, to=att)
        mx_rows = sb("mx_rows", [16, 2, D], F32R, to=att)
        rz = sb("rz", [128, D], to=att)
        at = sb("at", [128, 2, D], to=att)
        att.close()
        z = sb("z", [128, 2, 2, C])
        z_hi = sb("z_hi", [128, 2, 2, C], F32R)
        z_lo = sb("z_lo", [128, 2, 2, C], F32R)
        mask = sb("mask", [128, 4, C])
        silu = sb("silu", [128, 2, C])
        hid = sb("hid", [128, 2, C])
        h_hi = sb("h_hi", [128, 3, C], F32R)
        h_lo = sb("h_lo", [128, 3, C], F32R)
        low = sb("low", [128, 2, C])
        a_hi = sb("a_hi", [128, C], F32R)
        a_lo = sb("a_lo", [128, C], F32R)
        y_sb = sb("y_sb", [128, 2, 512])
        rev = sb("rev", [128, B, E])
        lg = sb("lg", [128, B, E])
        pr = sb("pr", [128, B, E])
        pr2 = sb("pr2", [128, B, E])
        oh = sb("oh", [128, 2, B, E])
        tmp = sb("tmp", [128, B, E])
        mcol = sb("mcol", [128, 8, B])
        sels = sb("sels", [128, 4, B, E])
        wide = sb("wide", [128, 4, B, E, RANK])

        s_x = [sem(f"s_x{b}") for b in range(B)]
        s_ctx = [sem(f"s_ctx{i}") for i in range(2)]
        s_ctxT = [sem(f"s_ctxT{i}") for i in range(2)]
        s_sel = sem("s_sel")
        s_w = [sem(f"s_w{i}") for i in range(WPARTS)]
        c_ident = sem("c_ident")
        c_ones = sem("c_ones")
        c_vzero = sem("c_vzero")
        c_qzero = sem("c_qzero")
        c_rev = sem("c_rev")
        c_sel = sem("c_sel")
        ln_stat = sem("ln_stat")
        ln_step = sem("ln_step")
        qf_ready = sem("qf_ready")
        hi_q = sem("hi_q")
        hi_k = sem("hi_k")
        lo_q = sem("lo_q")
        lo_k = sem("lo_k")
        v_ready = sem("v_ready")
        wrote_q = [sem(f"wrote_q{i}") for i in range(2)]
        wrote_k = [sem(f"wrote_k{i}") for i in range(2)]
        q_loaded = [sem(f"q_loaded{i}") for i in range(NQ)]
        k_loaded = [sem(f"k_loaded{i}") for i in range(NQ)]
        s_ready = sem("s_ready")
        max_done = sem("max_done")
        mx_hi = sem("mx_hi")
        mx_lo = sem("mx_lo")
        mt_ready = sem("mt_ready")
        mt_copied = sem("mt_copied")
        rows_loaded = [sem(f"rows_loaded{i}") for i in range(2)]
        st_ready = sem("st_ready")
        exp_done = sem("exp_done")
        uz_done = sem("uz_done")
        rz_done = sem("rz_done")
        at_done = sem("at_done")
        x1_done = sem("x1_done")
        w_hi_done = sem("w_hi_done")
        w_lo_done = sem("w_lo_done")
        ln2_stat = sem("ln2_stat")
        ln2_step = sem("ln2_step")
        xn_done = sem("xn_done")
        xT_ready = sem("xT_ready")
        xT_hi_done = sem("xT_hi_done")
        xT_lo_done = sem("xT_lo_done")
        r_ready = sem("r_ready")
        r_step = sem("r_step")
        r_exp = sem("r_exp")
        wide_first = sem("wide_first")
        wide_rest = sem("wide_rest")
        mask_ready = sem("mask_ready")
        mask_copied = sem("mask_copied")
        z_ready = sem("z_ready")
        z_masked = sem("z_masked")
        z_hi_done = sem("z_hi_done")
        z_lo_done = sem("z_lo_done")
        gu_ready = sem("gu_ready")
        silu_done = sem("silu_done")
        hid_done = sem("hid_done")
        h_hi_done = sem("h_hi_done")
        h_lo_done = sem("h_lo_done")
        down_done = sem("down_done")
        low_done = sem("low_done")
        low_sum = sem("low_sum")
        a_hi_done = sem("a_hi_done")
        a_lo_done = sem("a_lo_done")
        o_ready = sem("o_ready")
        y_done = sem("y_done")
        s_out = [sem(f"s_out{i}") for i in range(2)]

        block = ctx.enter_context(nc.Block())

        def W(part, name, at_col, n):
            a = AT[name] + at_col
            return (w_hi, w_lo)[part][:, a:a + n]

        PASSES = [(0, 0), (1, 0), (0, 1)]

        STAGES = [(m, kind) for m0 in range(0, MT, 2) for kind in range(3) for m in (m0, m0 + 1)]
        NS = len(STAGES)

        SELECTED = 18

        def repeated(i, c):
            return sels[:, i, TC * c:TC * (c + 1), :].rearrange("p t (e a) -> p (t e) a", a=1)\
                .to_broadcast([128, TC * E, RANK])

        @block.sync
        def _(sp):
            sp.dma_start(x_sb[:, 0, :], xv[:, 0, :]).then_inc(s_x[0], 16)
            sp.dma_start(x_sb[:, 1, :], xv[:, 1, :]).then_inc(s_x[1], 16)
            sp.dma_start(c_sb[:, 0:2, :], cv[:, 0:2, :]).then_inc(s_ctx[0], 16)
            for b in range(2, B):
                sp.dma_start(x_sb[:, b, :], xv[:, b, :]).then_inc(s_x[b], 16)
            sp.dma_start(sel_sb[MAXROW:MAXROW + 16, :, :], sel).then_inc(s_sel, 16)
            sp.dma_start(ct_sb[:, 0:2, :, :], tv[:, 0:2, :, :]).then_inc(s_ctxT[0], 16)

            def stack(b):
                r, n = b % 2, b % NQ
                sp.wait_ge(lo_k, b + 1)
                sp.dma_start(scratch[b, 2:4].rearrange("t p m -> p t m"), split[:, r, 2:4, :].bitcast(F32)).then_inc(wrote_k[r], 16)
                sp.wait_ge(lo_q, b + 1)
                sp.dma_start(scratch[b, 0:2].rearrange("t p m -> p t m"), split[:, r, 0:2, :].bitcast(F32)).then_inc(wrote_q[r], 16)
                if b >= NQ:
                    sp.wait_ge(st_ready, H * (b - NQ + 1))
                for t, wrote, dst, loaded, halves in ((2, wrote_k, K, k_loaded, (0, 0, 1, 1)),
                                                      (0, wrote_q, Q, q_loaded, (0, 1, 0, 1))):
                    sp.wait_ge(wrote[r], 16 * (b // 2 + 1))
                    for i, half in enumerate(halves):
                        sp.dma_start(dst[HD * i:HD * (i + 1), n, :, :].bitcast(F32),
                                     scratch[b, t + half].rearrange("(h d) m -> d h m", d=HD)).then_inc(loaded[n], 16)

            stack(0)
            sp.dma_start(c_sb[:, 2:B, :], cv[:, 2:B, :]).then_inc(s_ctx[1], 16)
            sp.dma_start(ct_sb[:, 2:B, :, :], tv[:, 2:B, :, :]).then_inc(s_ctxT[1], 16)
            w = 0
            for b in range(1, B):
                stack(b)
                for _ in range(2):
                    if w < WPARTS:
                        if w >= 2:
                            sp.wait_ge(w_lo_done, w - 1)
                        sp.dma_start(w_raw[:, w % 2, :], weights[:, w * WP:(w + 1) * WP]).then_inc(s_w[w], 16)
                        w += 1
            for c in range(NC):
                for o in range(2):
                    n = 2 * c + o
                    sp.wait_ge(y_done, n + 1)
                    sp.dma_start(ov[:, TC * c + 2 * o:TC * c + 2 * o + 2, :],
                                 y_sb[:, n % 2, :].rearrange("p (t d) -> p t d", d=D)).then_inc(s_out[n % 2], 16)
            sp.wait_ge(s_out[0], 16 * NC)
            sp.wait_ge(s_out[1], 16 * NC)

        @block.gpsimd
        def _(pool):
            def zero_rows(n):
                for i, buf in enumerate((Q, K)):
                    pool.memset(buf[64:96, n, :, :].bitcast(U32), 0).then_inc(c_qzero, 1)
                    pool.wait_ge(c_qzero, 2 * n + i + 1)

            zero_rows(0)
            pool.memset(V[:, :, :, :, :], 0.0).then_inc(c_vzero, 1)
            pool.memset(ones[:, :, :], 0.0).then_inc(c_ones, 1)
            pool.wait_ge(c_ones, 1)
            pool.memset(ones[:, 0, 0:16], 1.0)
            pool.memset(ones[:, 1, 16:32], 1.0).then_inc(c_ones, 1)
            pool.memset(ident[:, :], 0.0).then_inc(c_ident, 1)
            pool.wait_ge(c_ident, 1)
            pool.affine_select(out=ident[:, :], in_=ident[:, :], compare_op=ALU.not_equal, fill=1.0, base=0,
                               pattern=[[-1, 128]], channel_multiplier=1).then_inc(c_ident, 1)

            def lows(b):
                r = b % 2
                if b >= 2:
                    pool.wait_ge(wrote_k[r], 16 * (b // 2))
                    pool.wait_ge(wrote_q[r], 16 * (b // 2))
                pool.wait_ge(hi_k, b + 1)
                pool.tensor_tensor(split[:, r, 3, :], c_sb[:, b, :], split[:, r, 2, :].bitcast(F32),
                                   ALU.subtract).then_inc(lo_k, 1)
                pool.wait_ge(hi_q, b + 1)
                pool.tensor_tensor(split[:, r, 1, :], qf[:, r, :], split[:, r, 0, :].bitcast(F32),
                                   ALU.subtract).then_inc(lo_q, 1)

            def values(b):
                r = b % 2
                pool.wait_ge(s_ctxT[min(b // 2, 1)], 16)
                if b == 0:
                    pool.wait_ge(c_vzero, 1)
                if b >= 2:
                    pool.wait_ge(uz_done, 2 * (b - 1))
                src = ct_sb[:, b, :, :].rearrange("p k (g t c) -> p k g t c", t=2, c=HD)
                dst = V[:, r, :, :, :].rearrange("p k (g t) c -> p k g t c", t=2)
                pool.tensor_copy(dst[:, :, :, 0, 0:16], src[:, :, :, 0, :])
                pool.tensor_copy(dst[:, :, :, 1, 16:32], src[:, :, :, 1, :]).then_inc(v_ready, 1)

            def residual(b):
                pool.wait_ge(at_done, b + 1)
                pool.tensor_tensor(x1[:, b, :], x_sb[:, b, :], at[:, b % 2, :], ALU.add).then_inc(x1_done, 1)

            def weight(w):
                pool.wait_ge(s_w[w], 16)
                cols = slice(w * WP, (w + 1) * WP)
                pool.tensor_copy(w_hi[:, cols], w_raw[:, w % 2, :]).then_inc(w_hi_done, 1)
                pool.wait_ge(w_hi_done, w + 1)
                pool.tensor_tensor(w_lo[:, cols], w_raw[:, w % 2, :], w_hi[:, cols].bitcast(F32),
                                   ALU.subtract).then_inc(w_lo_done, 1)

            lows(0)
            values(0)
            lows(1)
            values(1)
            pool.wait_ge(v_ready, 2)
            zero_rows(1)
            lows(2)
            pool.wait_ge(lo_q, 3)
            zero_rows(2)
            w = 0
            for b in range(B):
                for _ in range(2):
                    if w < WPARTS:
                        weight(w)
                        w += 1
                if b + 3 < B:
                    lows(b + 3)
                residual(b)
                if b + 2 < B:
                    values(b + 2)
            for e in range(E):
                last = pool.memset(rev[:, :, e:e + 1], float(E - e))
            last.then_inc(c_rev, 1)
            pool.wait_ge(r_step, SELECTED)
            for i, c in [(2, 0), (3, 0)] + [(i, 1) for i in range(4)]:
                pool.tensor_copy(wide[:, i, TC * c:TC * (c + 1), :, :].rearrange("p t e r -> p (t e) r"),
                                 repeated(i, c)).then_inc(wide_rest, 1)

        @block.scalar
        def _(act):
            def highs(b):
                r = b % 2
                act.wait_ge(s_ctx[min(b // 2, 1)], 16)
                if b >= 2:
                    act.wait_ge(wrote_k[r], 16 * (b // 2))
                    act.wait_ge(wrote_q[r], 16 * (b // 2))
                act.activation(split[:, r, 2, :], c_sb[:, b, :], ACT.Copy).then_inc(hi_k, 1)
                act.wait_ge(qf_ready, b + 1)
                act.activation(split[:, r, 0, :], qf[:, r, :], ACT.Copy).then_inc(hi_q, 1)

            def max_rows(b):
                act.wait_ge(mt_ready, b + 1)
                if b >= 2:
                    act.wait_ge(rows_loaded[b % 2], 16 * (b // 2))
                act.activation(mx_rows[:, b % 2, :], MAX_BANK[0:16, 0:D], ACT.Copy).then_inc(mt_copied, 1)
                act.wait_ge(mt_copied, b + 1)
                if b >= NQ:
                    act.wait_ge(st_ready, H * (b - NQ + 1))
                act.dma_start(Q[MAXROW:MAXROW + 16, b % NQ, :, :].bitcast(F32),
                              mx_rows[:, b % 2, :].bitcast(F32).rearrange("p (a m) -> p a m", a=1).to_broadcast([16, H, D]))\
                    .then_inc(rows_loaded[b % 2], 16)

            def exps(b):
                for i in range(H):
                    n = H * b + i
                    act.wait_ge(st_ready, n + 1)
                    if n >= H:
                        act.wait_ge(uz_done, n // 4 - 1)
                    act.activation(P[:, n % H, :, :], ST_BANK[n % 2][:, :], ACT.Exp, scale=SCALE).then_inc(exp_done, 1)

            highs(0)
            highs(1)
            highs(2)
            act.wait_ge(s_sel, 16)
            for n in range(NQ):
                act.activation(K[MAXROW:MAXROW + 16, n, :, :], sel_sb[MAXROW:MAXROW + 16, :, :], ACT.Copy)\
                    .then_inc(c_sel, 1)
            max_rows(0)
            for b in range(B):
                exps(b)
                if b + 1 < B:
                    max_rows(b + 1)
                if b + 3 < B:
                    highs(b + 3)
            for b in range(B):
                act.wait_ge(xT_ready, b + 1)
                act.activation(xT_hi[:, :, b * 128:(b + 1) * 128],
                               bank[b % 4][:, 0:D].rearrange("p (k t) -> p k t", k=KD), ACT.Copy).then_inc(xT_hi_done, 1)
            act.wait_ge(r_step, 2)
            act.activation(pr[:, :, :], lg[:, :, :], ACT.Exp).then_inc(r_exp, 1)

            def masks(c, i):
                n = 4 * c + i
                act.wait_ge(mask_ready, n + 1)
                if c >= 1 and i < 2:
                    act.wait_ge(z_masked, 4 * c)
                if c >= 1 and i >= 2:
                    act.wait_ge(low_done, 2 * c)
                act.activation(mask[:, i, :], O_BANK[i % 2][:, :], ACT.Copy).then_inc(mask_copied, 1)

            def stage_act(c, i):
                m, kind = STAGES[i]
                n = NS * c + i
                p = TAIL if m == MT - 1 else 128
                act.wait_ge(gu_ready, n + 1)
                if n >= 2:
                    act.wait_ge(hid_done, n - 1)
                act.activation(silu[0:p, n % 2, :], GU_BANK[m % 2][0][0:p, :], ACT.Silu).then_inc(silu_done, 1)

            def high_h(c, i):
                m, kind = STAGES[i]
                n = NS * c + i
                p = TAIL if m == MT - 1 else 128
                act.wait_ge(hid_done, n + 1)
                if n >= 3:
                    act.wait_ge(down_done, n - 2)
                act.activation(h_hi[0:p, n % 3, :], hid[0:p, n % 2, :], ACT.Copy).then_inc(h_hi_done, 1)

            for c in range(NC):
                for i in range(4):
                    masks(c, i)
                stage_act(c, 0)
                stage_act(c, 1)
                for i in range(4):
                    act.wait_ge(z_masked, 4 * c + i + 1)
                    if c >= 1:
                        act.wait_ge(gu_ready, NS * c)
                    act.activation(z_hi[:, i // 2, i % 2, :], z[:, i // 2, i % 2, :], ACT.Copy).then_inc(z_hi_done, 1)
                    if i < 2:
                        high_h(c, i)
                for i in range(2, NS):
                    stage_act(c, i)
                    high_h(c, i)
                act.wait_ge(low_sum, c + 1)
                if c >= 1:
                    act.wait_ge(o_ready, 2 * c)
                act.activation(a_hi[:, :], low[:, 0, :], ACT.Copy).then_inc(a_hi_done, 1)

        @block.tensor
        def _(pe):
            def scores(b, i):
                n, q, h = H * b + i, b % NQ, ORDER[i]
                if i == 0:
                    if b < NQ:
                        pe.wait_ge(c_qzero, 2 * b + 2)
                    pe.wait_ge(k_loaded[q], 64 * (b // NQ + 1))
                    pe.wait_ge(q_loaded[q], 64 * (b // NQ + 1))
                if n >= 2:
                    pe.wait_ge(max_done, n - 1)
                for mh in range(2):
                    mm = pe.matmul(S_BANK[n % 2][:, mh * D:(mh + 1) * D], Q[0:96, q, h, mh * 128:(mh + 1) * 128],
                                   K[0:96, q, h, :], start=True, stop=True)
                mm.then_inc(s_ready, 1)

            def scoresT(b, i):
                n, q, h = H * b + i, b % NQ, ORDER[i]
                if i == 0:
                    if b < NQ:
                        pe.wait_ge(c_sel, b + 1)
                    pe.wait_ge(rows_loaded[b % 2], 16 * (b // 2 + 1))
                if n >= 2:
                    pe.wait_ge(exp_done, n - 1)
                rows = MAXROW + 16
                for nh in range(2):
                    mm = pe.matmul(ST_BANK[n % 2][:, nh * D:(nh + 1) * D], K[0:rows, q, h, nh * 128:(nh + 1) * 128],
                                   Q[0:rows, q, h, :], start=True, stop=True)
                mm.then_inc(st_ready, 1)

            def max_rows(b):
                pe.wait_ge(mx_lo, b + 1)
                if b >= 1:
                    pe.wait_ge(mt_copied, b)
                for mh in range(2):
                    mm = pe.matmul(MAX_BANK[0:16, mh * 128:(mh + 1) * 128],
                                   mx_split[:, b % 2, mh, :, :].bitcast(F32).rearrange("p a h -> p (a h)"),
                                   ident[:, :], start=True, stop=True)
                mm.then_inc(mt_ready, 1)

            def pv(b, s):
                pe.wait_ge(exp_done, H * b + 4 * (s + 1))
                if s == 0:
                    pe.wait_ge(v_ready, b + 1)
                    if b >= 1:
                        pe.wait_ge(at_done, b)
                for nh in range(2):
                    for p in range(4):
                        q = P[:, 4 * s + p, nh, :]
                        first, last = s == 0 and nh == 0, s == 1 and nh == 1
                        pe.matmul(U_BANK[32 * p:32 * p + 32, 0:D], V[:, b % 2, nh, 2 * p + s, :], q,
                                  start=first, stop=last)
                    for p in range(4):
                        q = P[:, 4 * s + p, nh, :]
                        mm = pe.matmul(Z_BANK[32 * p:32 * p + 32, 0:D], ones[:, s, :], q,
                                       start=first, stop=last)
                mm.then_inc(uz_done, 1)

            pe.wait_ge(c_ident, 2)
            pe.wait_ge(c_ones, 2)
            for i in range(H):
                scores(0, i)
            max_rows(0)
            for b in range(B):
                more = b + 1 < B
                if more:
                    scores(b + 1, 0)
                    scores(b + 1, 1)
                for i in range(H):
                    scoresT(b, i)
                    if more and i + 2 < H:
                        scores(b + 1, i + 2)
                    if i == 5:
                        pv(b, 0)
                if more:
                    max_rows(b + 1)
                pv(b, 1)

            for b in range(B):
                pe.wait_ge(xn_done, b + 1)
                if b >= 4:
                    pe.wait_ge(xT_lo_done, b - 3)
                    pe.wait_ge(xT_hi_done, b - 3)
                for k in range(KD):
                    mm = pe.transpose(bank[b % 4][:, k * 128:(k + 1) * 128], xn2[:, b % 2, k * 128:(k + 1) * 128],
                                      ident[:, :])
                mm.then_inc(xT_ready, 1)

            xT = (xT_hi, xT_lo)
            pe.wait_ge(w_lo_done, WPARTS)
            pe.wait_ge(xT_hi_done, B)
            pe.wait_ge(xT_lo_done, B)
            for t in range(B):
                for i, (wp, xp) in enumerate(PASSES):
                    for k in range(KD):
                        mm = pe.matmul(O_BANK[0][:, t * E:(t + 1) * E], xT[xp][:, k, t * 128:(t + 1) * 128],
                                       W(wp, "wr", k * E, E), start=(t == 0 and i == 0 and k == 0),
                                       stop=(i == 2 and k == KD - 1), skip_group_check=True)
            mm.then_inc(r_ready, 1)

            def z_rows(c):
                if c >= 1:
                    pe.wait_ge(low_done, 2 * c)
                for j, name in enumerate(("ag", "au")):
                    for i, (wp, xp) in enumerate(PASSES):
                        for k in range(KD):
                            mm = pe.matmul(D_BANK[j][:, :], W(wp, name, k * 128, 128), xT[xp][:, k, c * C:(c + 1) * C],
                                           start=(i == 0 and k == 0), stop=(i == 2 and k == KD - 1))
                    mm.then_inc(z_ready, 1)

            def stage(c, i):
                m, kind = STAGES[i]
                n = NS * c + i
                g, u = GU_BANK[m % 2]
                if n >= 2:
                    pe.wait_ge(hid_done, n - 1)
                if i == 2:
                    pe.wait_ge(z_hi_done, 4 * c + 4)
                    pe.wait_ge(z_lo_done, 4 * c + 4)
                tail = m == MT - 1
                if kind == 0:
                    for wp, xp in PASSES:
                        for k in range(KD):
                            rhs = xT[xp][:, k, c * C:(c + 1) * C]
                            first = (wp, xp, k) == (0, 0, 0)
                            mm = pe.matmul(g[:, :], W(wp, "wg", (k * MT + m) * 128, 128), rhs,
                                           start=first, stop=False, skip_group_check=True)
                            if not tail:
                                mm = pe.matmul(u[:, :], W(wp, "wu", (k * (MT - 1) + m) * 128, 128), rhs,
                                               start=first, stop=False, skip_group_check=True)
                else:
                    for j, (name, to) in enumerate((("bg", g), ("bu", g if tail else u))):
                        for wp, xp in PASSES:
                            mm = pe.matmul(to[:, :], W(wp, name, m * 128, 128), (z_hi, z_lo)[xp][:, j, kind - 1, :],
                                           start=False, stop=(kind == 2), skip_group_check=True)
                mm.then_inc(gu_ready, 1)

            def down(c, i):
                m, kind = STAGES[i]
                n = NS * c + i
                s = n % 3
                pe.wait_ge(h_hi_done, n + 1)
                pe.wait_ge(h_lo_done, n + 1)
                passes = [(0, h_hi), (1, h_hi)] if m == MT - 1 else [(0, h_hi), (1, h_hi), (0, h_lo)]
                for j, (wp, h) in enumerate(passes):
                    if kind == 0:
                        for t in range(TC):
                            mm = pe.matmul(O_BANK[t // 2][:, (t % 2) * D:(t % 2 + 1) * D],
                                           h[:, s, t * 128:(t + 1) * 128], W(wp, "wd", m * D, D),
                                           start=(m == 0 and j == 0 and t % 2 == 0), stop=False, skip_group_check=True)
                    else:
                        mm = pe.matmul(D_BANK[kind - 1][:, :], W(wp, "ad", m * 128, 128), h[:, s, :],
                                       start=(m == 0 and j == 0), stop=(m == MT - 1 and j == len(passes) - 1))
                mm.then_inc(down_done, 1)

            def masks(c, i):
                n = 4 * c + i
                if i < 2 and c == 0:
                    pe.wait_ge(wide_first, i + 1)
                if i == 2 and c == 0:
                    pe.wait_ge(wide_rest, 2)
                if i == 0 and c == 1:
                    pe.wait_ge(wide_rest, 6)
                if i >= 2:
                    pe.wait_ge(mask_copied, n - 1)
                if i < 2 and c >= 1:
                    pe.wait_ge(y_done, 2 * c)
                for t in range(TC):
                    src = wide[:, i, TC * c + t, :, :].rearrange("p e r -> p (e r)")
                    mm = pe.matmul(O_BANK[i % 2][:, t * 128:(t + 1) * 128], src, ident[:, :], start=True, stop=True)
                mm.then_inc(mask_ready, 1)

            for c in range(NC):
                z_rows(c)
                stage(c, 0)
                stage(c, 1)
                for i in range(4):
                    masks(c, i)
                pe.wait_ge(mask_copied, 4 * c + 4)
                for i in range(2, NS):
                    stage(c, i)
                    down(c, i - 2)
                down(c, NS - 2)
                down(c, NS - 1)
                pe.wait_ge(a_hi_done, c + 1)
                pe.wait_ge(a_lo_done, c + 1)
                for o in range(2):
                    for t in (2 * o, 2 * o + 1):
                        for wp, a in ((0, a_hi), (1, a_hi), (0, a_lo)):
                            mm = pe.matmul(O_BANK[o][:, (t % 2) * D:(t % 2 + 1) * D], a[:, t * 128:(t + 1) * 128],
                                           W(wp, "bd", 0, D), start=False, stop=True, skip_group_check=True)
                    mm.then_inc(o_ready, 1)

        @block.vector
        def _(dve):
            def low_x(b):
                dve.wait_ge(xT_hi_done, b + 1)
                cols = slice(b * 128, (b + 1) * 128)
                dve.tensor_tensor(xT_lo[:, :, cols], bank[b % 4][:, 0:D].rearrange("p (k t) -> p k t", k=KD),
                                  xT_hi[:, :, cols].bitcast(F32), ALU.subtract).then_inc(xT_lo_done, 1)

            def rsqrt(which, b0, b1, done, at_least):
                cols = slice(b0, b1)
                v, t, y = nr_v[:, cols], nr_t[:, cols], rstd[:, which, cols]
                steps = [lambda: dve.tensor_scalar(v, mv[:, which, cols, 1], EPS, None, ALU.add),
                         lambda: dve.tensor_scalar(y.bitcast(U32), v.bitcast(U32), 1, None, ALU.logical_shift_right),
                         lambda: dve.tensor_scalar(y.bitcast(I32), y.bitcast(I32), -1, RSQRT_SEED, ALU.mult, ALU.add)]
                for _ in range(3):
                    steps += [lambda: dve.scalar_tensor_tensor(out=t, in0=y, scalar=-0.5, in1=y, op0=ALU.mult, op1=ALU.mult),
                              lambda: dve.tensor_tensor(t, t, v, ALU.mult),
                              lambda: dve.scalar_tensor_tensor(out=y, in0=t, scalar=1.5, in1=y, op0=ALU.add, op1=ALU.mult)]
                for n, step in enumerate(steps):
                    step().then_inc(done, 1)
                    dve.wait_ge(done, at_least + n + 1)
                return at_least + len(steps)

            def ln1_stats(b):
                dve.wait_ge(s_x[b], 16)
                dve.bn_stats(stats[:, 0, b, :], x_sb[:, b, :]).then_inc(ln_stat, 1)
                dve.wait_ge(ln_stat, 2 * b + 1)
                dve.bn_aggr(mv[:, 0, b, :], stats[:, 0, b, :]).then_inc(ln_stat, 1)

            def q_full(b):
                if b >= 2:
                    dve.wait_ge(lo_q, b - 1)
                dve.tensor_scalar(qf[:, b % 2, :], x_sb[:, b, :], mv[:, 0, b, 0:1], rstd[:, 0, b:b + 1],
                                  ALU.subtract, ALU.mult).then_inc(qf_ready, 1)

            def maxima(b, i):
                n = H * b + i
                dve.wait_ge(s_ready, n + 1)
                if i == 0 and b >= 2:
                    dve.wait_ge(mx_lo, b - 1)
                dve.tensor_reduce(mx[:, b % 2, :, ORDER[i]], S_BANK[n % 2][:, :].rearrange("p (a n) -> p a n", a=2),
                                  AX.X, ALU.max).then_inc(max_done, 1)

            def max_split(b):
                r = b % 2
                dve.wait_ge(max_done, H * (b + 1))
                if b >= 2:
                    dve.wait_ge(mt_ready, b - 1)
                dve.tensor_copy(mx_split[:, r, :, 0, :], mx[:, r, :, :]).then_inc(mx_hi, 1)
                dve.wait_ge(mx_hi, b + 1)
                dve.tensor_tensor(mx_split[:, r, :, 1, :], mx[:, r, :, :], mx_split[:, r, :, 0, :].bitcast(F32),
                                  ALU.subtract).then_inc(mx_lo, 1)

            def norm(b):
                dve.wait_ge(uz_done, 2 * (b + 1))
                dve.reciprocal(rz[:, :], Z_BANK[:, 0:D]).then_inc(rz_done, 1)
                dve.wait_ge(rz_done, b + 1)
                if b >= 2:
                    dve.wait_ge(x1_done, b - 1)
                dve.tensor_tensor(at[:, b % 2, :], U_BANK[:, 0:D], rz[:, :], ALU.mult).then_inc(at_done, 1)

            def ln2_stats(b):
                dve.wait_ge(x1_done, b + 1)
                dve.bn_stats(stats[:, 1, b, :], x1[:, b, :]).then_inc(ln2_stat, 1)
                dve.wait_ge(ln2_stat, 2 * b + 1)
                dve.bn_aggr(mv[:, 1, b, :], stats[:, 1, b, :]).then_inc(ln2_stat, 1)

            ln1_stats(0)
            ln1_stats(1)
            dve.wait_ge(ln_stat, 4)
            at_step = rsqrt(0, 0, 2, ln_step, 0)
            q_full(0)
            q_full(1)
            for b in range(2, B):
                ln1_stats(b)
            dve.wait_ge(ln_stat, 2 * B)
            rsqrt(0, 2, B, ln_step, at_step)
            q_full(2)
            for i in range(H):
                maxima(0, i)
            max_split(0)
            for b in range(B):
                if b + 1 < B:
                    for i in range(H):
                        maxima(b + 1, i)
                    max_split(b + 1)
                if b + 3 < B:
                    q_full(b + 3)
                if b >= 1:
                    ln2_stats(b - 1)
                norm(b)
            ln2_stats(B - 1)
            dve.wait_ge(ln2_stat, 2 * B)
            rsqrt(1, 0, B, ln2_step, 0)
            for b in range(B):
                if b >= 2:
                    dve.wait_ge(xT_ready, b - 1)
                dve.tensor_scalar(xn2[:, b % 2, :], x1[:, b, :], mv[:, 1, b, 0:1], rstd[:, 1, b:b + 1],
                                  ALU.subtract, ALU.mult).then_inc(xn_done, 1)
                if b >= 1:
                    low_x(b - 1)
            low_x(B - 1)

            step = [0]

            def done(ins):
                step[0] += 1
                ins.then_inc(r_step, 1)
                dve.wait_ge(r_step, step[0])

            def col(i):
                return mcol[:, i, :].rearrange("p (t a) -> p t a", a=1).to_broadcast([128, B, E])

            dve.wait_ge(r_ready, 1)
            dve.wait_ge(c_rev, 1)
            logits = O_BANK[0][:, 0:B * E].rearrange("p (t e) -> p t e", e=E)
            done(dve.tensor_reduce(mcol[:, 0, :], logits, AX.X, ALU.max))
            done(dve.tensor_tensor(lg[:, :, :], logits, col(0), ALU.subtract))
            dve.wait_ge(r_exp, 1)
            done(dve.tensor_reduce(mcol[:, 1, :], pr[:, :, :], AX.X, ALU.add))
            done(dve.reciprocal(mcol[:, 2, :], mcol[:, 1, :]))
            done(dve.tensor_tensor(pr2[:, :, :], pr[:, :, :], col(2), ALU.mult))
            for k in range(2):
                done(dve.tensor_reduce(mcol[:, 3 + k, :], pr2[:, :, :], AX.X, ALU.max))
                done(dve.tensor_tensor(tmp[:, :, :], pr2[:, :, :], col(3 + k), ALU.is_ge))
                done(dve.tensor_tensor(tmp[:, :, :], tmp[:, :, :], rev[:, :, :], ALU.mult))
                done(dve.tensor_reduce(mcol[:, 5 + k, :], tmp[:, :, :], AX.X, ALU.max))
                done(dve.tensor_tensor(oh[:, k, :, :], rev[:, :, :], col(5 + k), ALU.is_equal))
                if k == 0:
                    done(dve.scalar_tensor_tensor(out=pr2[:, :, :], in0=oh[:, 0, :, :], scalar=-2.0, in1=pr2[:, :, :],
                                                  op0=ALU.mult, op1=ALU.add))
            dve.tensor_scalar(sels[:, 0, :, :], oh[:, 0, :, :], LORA, None, ALU.mult)
            dve.tensor_tensor(sels[:, 1, :, :], oh[:, 1, :, :], oh[:, 0, :, :], ALU.subtract)
            for k in range(2):
                last = dve.scalar_tensor_tensor(out=sels[:, 2 + k, :, :], in0=oh[:, k, :, :], scalar=LORA, in1=col(3 + k),
                                                op0=ALU.mult, op1=ALU.mult)
            done(last)
            done(dve.tensor_scalar(sels[:, 1, :, :], sels[:, 1, :, :], LORA, None, ALU.mult))
            assert step[0] == SELECTED, step[0]
            for i in range(2):
                dve.tensor_copy(wide[:, i, 0:TC, :, :].rearrange("p t e r -> p (t e) r"),
                                repeated(i, 0)).then_inc(wide_first, 1)

            def gate(c, i):
                m, kind = STAGES[i]
                n = NS * c + i
                tail = m == MT - 1
                p = TAIL if tail else 128
                dve.wait_ge(silu_done, n + 1)
                if n >= 2:
                    dve.wait_ge(h_hi_done, n - 1)
                    dve.wait_ge(h_lo_done, n - 1)
                up = GU_BANK[m % 2][0][64:128, :] if tail else GU_BANK[m % 2][1][:, :]
                dve.tensor_tensor(hid[0:p, n % 2, :], silu[0:p, n % 2, :], up, ALU.mult).then_inc(hid_done, 1)

            def low_h(c, i):
                m, kind = STAGES[i]
                n = NS * c + i
                tail = m == MT - 1
                p = TAIL if tail else 128
                dve.wait_ge(h_hi_done, n + 1)
                dve.wait_ge(hid_done, n + 1)
                to = h_hi[64:128, n % 3, :] if tail else h_lo[:, n % 3, :]
                dve.tensor_tensor(to, hid[0:p, n % 2, :], h_hi[0:p, n % 3, :].bitcast(F32),
                                  ALU.subtract).then_inc(h_lo_done, 1)

            def z_mask(c, i):
                j, d = i // 2, i % 2
                dve.wait_ge(z_ready, 2 * c + j + 1)
                dve.wait_ge(mask_copied, 4 * c + d + 1)
                if c >= 1:
                    dve.wait_ge(z_hi_done, 4 * c)
                dve.tensor_tensor(z[:, j, d, :], D_BANK[j][:, :], mask[:, d, :], ALU.mult).then_inc(z_masked, 1)

            def z_low(c, i):
                j, d = i // 2, i % 2
                dve.wait_ge(z_hi_done, 4 * c + i + 1)
                dve.tensor_tensor(z_lo[:, j, d, :], z[:, j, d, :], z_hi[:, j, d, :].bitcast(F32),
                                  ALU.subtract).then_inc(z_lo_done, 1)

            for c in range(NC):
                gate(c, 0)
                gate(c, 1)
                for i in range(4):
                    z_mask(c, i)
                for i in range(4):
                    z_low(c, i)
                    if i < 2:
                        low_h(c, i)
                for i in range(2, NS):
                    gate(c, i)
                    low_h(c, i)
                dve.wait_ge(down_done, NS * (c + 1))
                if c >= 1:
                    dve.wait_ge(a_hi_done, c)
                for k in range(2):
                    dve.tensor_tensor(low[:, k, :], D_BANK[k][:, :], mask[:, 2 + k, :], ALU.mult).then_inc(low_done, 1)
                dve.wait_ge(low_done, 2 * c + 2)
                dve.tensor_tensor(low[:, 0, :], low[:, 0, :], low[:, 1, :], ALU.add).then_inc(low_sum, 1)
                dve.wait_ge(a_hi_done, c + 1)
                if c >= 1:
                    dve.wait_ge(o_ready, 2 * c)
                dve.tensor_tensor(a_lo[:, :], low[:, 0, :], a_hi[:, :].bitcast(F32), ALU.subtract).then_inc(a_lo_done, 1)
                for o in range(2):
                    n = 2 * c + o
                    dve.wait_ge(o_ready, n + 1)
                    if c >= 1:
                        dve.wait_ge(s_out[o], 16 * c)
                    b = TC * c + 2 * o
                    dve.tensor_tensor(y_sb[:, o, :], x1[:, b:b + 2, :].rearrange("p b d -> p (b d)"), O_BANK[o][:, :],
                                      ALU.add).then_inc(y_done, 1)


_OUTS = [((8, 128, 256), "float32")]


def kernel(**inputs):
    import numpy as _np
    import concourse.bacc as _bacc
    from concourse import mybir as _mybir
    from concourse.bass_utils import run_bass_kernel_spmd as _run

    a = {k: _np.ascontiguousarray(v) for k, v in inputs.items()}
    ctx_in = a["ctx_2048"]

    def tiles(m, width):
        k = m.shape[0] // 128
        o = _np.zeros((128, k, width), m.dtype)
        o[:, :, :m.shape[1]] = m.reshape(k, 128, m.shape[1]).transpose(1, 0, 2)
        return o.reshape(128, k * width)

    full, tail = (MT - 1) * 128, TAIL
    wg, wu = a["L0_ffn_Wg"].T, a["L0_ffn_Wu"].T
    wg_l = _np.concatenate([wg, wu[:, full:]], axis=1)
    wu_l = wu[:, :full]
    ag = a["L0_ffn_Ag"].reshape(E * RANK, D).T
    au = a["L0_ffn_Au"].reshape(E * RANK, D).T
    bg = a["L0_ffn_Bg"].transpose(0, 2, 1).reshape(E * RANK, F)
    bu = a["L0_ffn_Bu"].transpose(0, 2, 1).reshape(E * RANK, F)
    pad = _np.zeros((E * RANK, tail), bg.dtype)
    bg_l = _np.concatenate([bg, pad], axis=1)
    bu_l = _np.concatenate([bu[:, :full], pad, bu[:, full:]], axis=1)

    def twice_tail(m):
        return tiles(_np.concatenate([m, m[full:]], axis=0), m.shape[1])

    wd_l = twice_tail(a["L0_ffn_Wd"].T)
    ad_l = twice_tail(a["L0_ffn_Ad"].reshape(E * RANK, F).T)
    bd_l = a["L0_ffn_Bd"].transpose(0, 2, 1).reshape(E * RANK, D)
    parts = {"wg": tiles(wg_l, MT * 128), "wu": tiles(wu_l, (MT - 1) * 128), "ag": tiles(ag, 128), "au": tiles(au, 128),
             "wr": tiles(a["L0_ffn_Wr"].T, E), "bg": bg_l, "bu": bu_l, "wd": wd_l, "ad": ad_l, "bd": bd_l}
    weights = _np.concatenate([parts[name] for name, _ in PIECES], axis=1)
    sel = _np.zeros((2, H, H, D), _np.float32)
    for h in range(H):
        sel[:, h, h, :] = -1.0
    arrays = {
        "x": a["x"], "ctx_in": ctx_in, "ctxT": _np.ascontiguousarray(ctx_in.transpose(0, 2, 1)),
        "weights": _np.ascontiguousarray(weights), "sel": sel.reshape(2 * H, H, D),
    }
    nc = _bacc.Bacc("TRN2", target_bir_lowering=False, num_devices=1)
    args = [nc.dram_tensor(n, v.shape, _mybir.dt.from_np(v.dtype), kind="ExternalInput").ap() for n, v in arrays.items()]
    for i, (shape, dtype) in enumerate(_OUTS):
        args.append(nc.dram_tensor(f"out_{i}", shape, _mybir.dt.from_np(_np.dtype(dtype)), kind="ExternalOutput").ap())
    xattn_lora_ffn_kernel(nc, *args)
    r = _run(nc, [arrays], core_ids=[0])
    return r.results[0]["out_0"]
```

```python
from contextlib import ExitStack

import concourse.bass as bass
from concourse import mybir

F32 = mybir.dt.float32
F32R = mybir.dt.float32r
I32 = mybir.dt.int32
U32 = mybir.dt.uint32
ALU = mybir.AluOpType
ACT = mybir.ActivationFunctionType
AX = mybir.AxisListType

B, R, D = 8, 128, 256
H, HD = 8, 16
SCALE = float(HD) ** -0.5
F = 704
E, RANK = 8, 16
LORA = 2.0
EPS = 1e-5
NT = B * R
KD = D // 128
MT = (F + 127) // 128
TAIL = F - (MT - 1) * 128
C = 512
NC = NT // C
TC = C // 128
ORDER = [0, 2, 4, 6, 1, 3, 5, 7]
NQ = 3
MAXROW = 96
RSQRT_SEED = 0x5F3759DF
RSQRT_STEPS = 12

PIECES = [("wg", KD * MT * 128), ("wu", KD * (MT - 1) * 128), ("ag", KD * 128), ("au", KD * 128),
          ("wr", KD * E), ("bg", MT * 128), ("bu", MT * 128), ("wd", MT * D), ("ad", MT * 128), ("bd", D)]
AT = {}
NW = 0
for _name, _n in PIECES:
    AT[_name] = NW
    NW += _n
WPARTS = 10
WP = NW // WPARTS


def xattn_lora_ffn_kernel(nc, x, ctx_in, ctxT, weights, sel, out):
    xv = x.rearrange("b r d -> r b d")
    cv = ctx_in.rearrange("b r d -> r b d")
    tv = ctxT.rearrange("b (k p) r -> p b k r", p=128)
    ov = out.rearrange("b r d -> r b d")
    scratch = nc.dram_tensor("scratch", [B, 4, R, D], F32, kind="Internal").ap()

    with ExitStack() as ctx:
        def sb(name, shape, dt=F32, to=None):
            return (to or ctx).enter_context(nc.sbuf_tensor(name, shape, dt))

        def sem(name):
            return ctx.enter_context(nc.semaphore(name))

        bank = [ctx.enter_context(nc.psum_tensor(f"bank{i}", [128, 512], F32)) for i in range(8)]
        S_BANK, ST_BANK, MAX_BANK, UZ_BANK = [bank[0], bank[1], bank[7]], bank[2:4], bank[4], bank[5:7]
        GU_BANK, O_BANK, D_BANK = [bank[0:2], bank[2:4]], bank[4:6], bank[6:8]
        ROUTE_BANK = [bank[4], bank[3]]

        x_sb = sb("x_sb", [128, B, D])
        x1 = sb("x1", [128, B, D])
        w_hi = sb("w_hi", [128, NW], F32R)
        w_lo = sb("w_lo", [128, NW], F32R)
        w_raw = sb("w_raw", [128, 2, WP])
        ident = sb("ident", [128, 128])
        stats = sb("stats", [128, 2, B, 6])
        mv = sb("mv", [128, 2, B, 2])
        rstd = sb("rstd", [128, 2, B])
        nr_v = sb("nr_v", [128, B])
        nr_t = sb("nr_t", [128, B])
        xT_hi = sb("xT_hi", [128, KD, NT], F32R)
        xT_lo = sb("xT_lo", [128, KD, NT], F32R)
        xn2 = sb("xn2", [128, 4, D])

        sel_sb = x1

        att = ExitStack()
        c_sb = sb("c_sb", [128, B, D], to=att)
        ct_sb = sb("ct_sb", [128, B, 2, R], to=att)
        qf = sb("qf", [128, 2, D], to=att)
        split = sb("split", [128, 2, 4, D], F32R, to=att)
        Q = sb("Q", [128, NQ, H, D], F32R, to=att)
        K = sb("K", [128, NQ, H, D], F32R, to=att)
        V = sb("V", [128, 2, 2, H, 32], to=att)
        ones = sb("ones", [128, 2, 32], to=att)
        P = sb("P", [128, H, 2, D], to=att)
        mx = sb("mx", [128, 2, 2, H], to=att)
        mx_split = sb("mx_split", [128, 2, 2, 2, H], F32R, to=att)
        mx_rows = sb("mx_rows", [16, 2, D], F32R, to=att)
        rz = sb("rz", [128, D], to=att)
        at = sb("at", [128, 2, D], to=att)
        att.close()
        z_raw = sb("z_raw", [128, 2, C])
        z = sb("z", [128, 2, 2, C])
        z_hi = sb("z_hi", [128, NC, 2, 2, C], F32R)
        z_lo = sb("z_lo", [128, NC, 2, 2, C], F32R)
        weight_mask = sb("weight_mask", [128, NC, 2, C])
        silu = sb("silu", [128, 2, C])
        hid = sb("hid", [128, 3, C])
        h_hi = sb("h_hi", [128, 3, C], F32R)
        h_lo = sb("h_lo", [128, 3, C], F32R)
        low = sb("low", [128, 2, C])
        a_hi = sb("a_hi", [128, C], F32R)
        a_lo = sb("a_lo", [128, C], F32R)
        y_sb = sb("y_sb", [128, 2, 512])
        lT = sb("lT", [E, C])
        rev = sb("rev", [128, TC, E])
        lg = sb("lg", [128, TC, E])
        lg2 = sb("lg2", [128, TC, E])
        pr = sb("pr", [128, TC, E])
        tmp = sb("tmp", [128, TC, E])
        mcol = sb("mcol", [128, 6, TC])
        sels = sb("sels", [128, 4, TC, E])
        second = sb("second", [128, TC, E])
        wide = sb("wide", [128, 4, TC, E, RANK])

        s_x = [sem(f"s_x{b}") for b in range(B)]
        s_ctx = [sem(f"s_ctx{i}") for i in range(2)]
        s_ctxT = [sem(f"s_ctxT{i}") for i in range(2)]
        s_sel = sem("s_sel")
        s_w = [sem(f"s_w{i}") for i in range(WPARTS)]
        c_ident = sem("c_ident")
        c_ones = sem("c_ones")
        c_vzero = sem("c_vzero")
        c_qzero = sem("c_qzero")
        c_rev = sem("c_rev")
        c_sel = sem("c_sel")
        ln_stat = sem("ln_stat")
        ln_step = sem("ln_step")
        qf_ready = sem("qf_ready")
        hi_q = sem("hi_q")
        hi_k = sem("hi_k")
        lo_q = sem("lo_q")
        lo_k = sem("lo_k")
        v_ready = sem("v_ready")
        wrote_q = [sem(f"wrote_q{i}") for i in range(2)]
        wrote_k = [sem(f"wrote_k{i}") for i in range(2)]
        q_loaded = [sem(f"q_loaded{i}") for i in range(NQ)]
        k_loaded = [sem(f"k_loaded{i}") for i in range(NQ)]
        s_ready = sem("s_ready")
        max_done = sem("max_done")
        mx_hi = sem("mx_hi")
        mx_lo = sem("mx_lo")
        mt_ready = sem("mt_ready")
        mt_copied = sem("mt_copied")
        rows_loaded = [sem(f"rows_loaded{i}") for i in range(2)]
        st_ready = sem("st_ready")
        exp_done = sem("exp_done")
        uz_done = sem("uz_done")
        rz_done = sem("rz_done")
        at_done = sem("at_done")
        x1_done = sem("x1_done")
        w_hi_done = sem("w_hi_done")
        w_lo_done = sem("w_lo_done")
        ln2_stat = sem("ln2_stat")
        ln2_step = sem("ln2_step")
        xn_done = sem("xn_done")
        xT_ready = sem("xT_ready")
        xT_hi_done = sem("xT_hi_done")
        xT_lo_done = sem("xT_lo_done")
        lT_ready = sem("lT_ready")
        lT_copied = sem("lT_copied")
        logits_ready = sem("logits_ready")
        r_step = sem("r_step")
        r_exp = sem("r_exp")
        wide_first = sem("wide_first")
        wide_rest = sem("wide_rest")
        mask_ready = sem("mask_ready")
        mask_copied = sem("mask_copied")
        z_ready = sem("z_ready")
        z_copied = sem("z_copied")
        z_masked = sem("z_masked")
        z_hi_done = sem("z_hi_done")
        z_lo_done = sem("z_lo_done")
        gu_ready = sem("gu_ready")
        silu_done = sem("silu_done")
        hid_done = sem("hid_done")
        h_hi_done = sem("h_hi_done")
        h_lo_done = sem("h_lo_done")
        down_done = sem("down_done")
        low_done = sem("low_done")
        low_sum = sem("low_sum")
        a_hi_done = sem("a_hi_done")
        a_lo_done = sem("a_lo_done")
        o_ready = sem("o_ready")
        y_done = sem("y_done")
        s_out = [sem(f"s_out{i}") for i in range(2)]

        block = ctx.enter_context(nc.Block())

        def W(part, name, at_col, n):
            a = AT[name] + at_col
            return (w_hi, w_lo)[part][:, a:a + n]

        PASSES = [(0, 0), (1, 0), (0, 1)]

        STAGES = [(m, kind) for m0 in range(0, MT, 2) for kind in range(3) for m in (m0, m0 + 1)]
        NS = len(STAGES)

        READ, CHOSEN, SELECTED = 2, 12, 18

        def repeated(i):
            return sels[:, i, :, :].rearrange("p t (e a) -> p (t e) a", a=1).to_broadcast([128, TC * E, RANK])

        def wide_out(i):
            return wide[:, i, :, :, :].rearrange("p t e r -> p (t e) r")

        def pair(xT, p):
            return xT[:, :, 256 * p:256 * (p + 1)].rearrange("p k (b t) -> p b k t", b=2)

        def turned(p):
            bk = MAX_BANK if p < 2 else bank[7]
            return bk[:, :].rearrange("p (b k t) -> p b k t", b=2, k=KD)

        @block.sync
        def _(sp):
            sp.dma_start(x_sb[:, 0, :], xv[:, 0, :]).then_inc(s_x[0], 16)
            sp.dma_start(x_sb[:, 1, :], xv[:, 1, :]).then_inc(s_x[1], 16)
            sp.dma_start(c_sb[:, 0:2, :], cv[:, 0:2, :]).then_inc(s_ctx[0], 16)
            for b in range(2, B):
                sp.dma_start(x_sb[:, b, :], xv[:, b, :]).then_inc(s_x[b], 16)
            sp.dma_start(sel_sb[MAXROW:MAXROW + 16, :, :], sel).then_inc(s_sel, 16)
            sp.dma_start(ct_sb[:, 0:2, :, :], tv[:, 0:2, :, :]).then_inc(s_ctxT[0], 16)

            def stack(b):
                r, n = b % 2, b % NQ
                sp.wait_ge(lo_k, b + 1)
                sp.dma_start(scratch[b, 2:4].rearrange("t p m -> p t m"), split[:, r, 2:4, :].bitcast(F32)).then_inc(wrote_k[r], 16)
                sp.wait_ge(lo_q, b + 1)
                sp.dma_start(scratch[b, 0:2].rearrange("t p m -> p t m"), split[:, r, 0:2, :].bitcast(F32)).then_inc(wrote_q[r], 16)
                if b >= NQ:
                    sp.wait_ge(st_ready, H * (b - NQ + 1))
                for t, wrote, dst, loaded, halves in ((2, wrote_k, K, k_loaded, (0, 0, 1, 1)),
                                                      (0, wrote_q, Q, q_loaded, (0, 1, 0, 1))):
                    sp.wait_ge(wrote[r], 16 * (b // 2 + 1))
                    for i, half in enumerate(halves):
                        sp.dma_start(dst[HD * i:HD * (i + 1), n, :, :].bitcast(F32),
                                     scratch[b, t + half].rearrange("(h d) m -> d h m", d=HD)).then_inc(loaded[n], 16)

            stack(0)
            sp.dma_start(c_sb[:, 2:B, :], cv[:, 2:B, :]).then_inc(s_ctx[1], 16)
            sp.dma_start(ct_sb[:, 2:B, :, :], tv[:, 2:B, :, :]).then_inc(s_ctxT[1], 16)
            w = 0
            for b in range(1, B):
                stack(b)
                for _ in range(2):
                    if w < WPARTS:
                        if w >= 2:
                            sp.wait_ge(w_lo_done, w - 1)
                        sp.dma_start(w_raw[:, w % 2, :], weights[:, w * WP:(w + 1) * WP]).then_inc(s_w[w], 16)
                        w += 1
            for c in range(NC):
                for o in range(2):
                    n = 2 * c + o
                    sp.wait_ge(y_done, n + 1)
                    sp.dma_start(ov[:, TC * c + 2 * o:TC * c + 2 * o + 2, :],
                                 y_sb[:, n % 2, :].rearrange("p (t d) -> p t d", d=D)).then_inc(s_out[n % 2], 16)
            sp.wait_ge(s_out[0], 16 * NC)
            sp.wait_ge(s_out[1], 16 * NC)

        @block.gpsimd
        def _(pool):
            def zero_rows(n):
                for i, buf in enumerate((Q, K)):
                    pool.memset(buf[64:96, n, :, :].bitcast(U32), 0).then_inc(c_qzero, 1)
                    pool.wait_ge(c_qzero, 2 * n + i + 1)

            zero_rows(0)
            pool.memset(V[:, :, :, :, :], 0.0).then_inc(c_vzero, 1)
            pool.memset(ones[:, :, :], 0.0).then_inc(c_ones, 1)
            pool.wait_ge(c_ones, 1)
            pool.memset(ones[:, 0, 0:16], 1.0)
            pool.memset(ones[:, 1, 16:32], 1.0).then_inc(c_ones, 1)
            pool.memset(ident[:, :], 0.0).then_inc(c_ident, 1)
            pool.wait_ge(c_ident, 1)
            pool.affine_select(out=ident[:, :], in_=ident[:, :], compare_op=ALU.not_equal, fill=1.0, base=0,
                               pattern=[[-1, 128]], channel_multiplier=1).then_inc(c_ident, 1)

            def lows(b):
                r = b % 2
                if b >= 2:
                    pool.wait_ge(wrote_k[r], 16 * (b // 2))
                    pool.wait_ge(wrote_q[r], 16 * (b // 2))
                pool.wait_ge(hi_k, b + 1)
                pool.tensor_tensor(split[:, r, 3, :], c_sb[:, b, :], split[:, r, 2, :].bitcast(F32),
                                   ALU.subtract).then_inc(lo_k, 1)
                pool.wait_ge(hi_q, b + 1)
                pool.tensor_tensor(split[:, r, 1, :], qf[:, r, :], split[:, r, 0, :].bitcast(F32),
                                   ALU.subtract).then_inc(lo_q, 1)

            def values(b):
                r = b % 2
                pool.wait_ge(s_ctxT[min(b // 2, 1)], 16)
                if b == 0:
                    pool.wait_ge(c_vzero, 1)
                if b >= 2:
                    pool.wait_ge(uz_done, 2 * (b - 1))
                src = ct_sb[:, b, :, :].rearrange("p k (g t c) -> p k g t c", t=2, c=HD)
                dst = V[:, r, :, :, :].rearrange("p k (g t) c -> p k g t c", t=2)
                pool.tensor_copy(dst[:, :, :, 0, 0:16], src[:, :, :, 0, :])
                pool.tensor_copy(dst[:, :, :, 1, 16:32], src[:, :, :, 1, :]).then_inc(v_ready, 1)

            def residual(b):
                pool.wait_ge(at_done, b + 1)
                if b == 0:
                    pool.wait_ge(c_sel, NQ)
                pool.tensor_tensor(x1[:, b, :], x_sb[:, b, :], at[:, b % 2, :], ALU.add).then_inc(x1_done, 1)

            def weight(w):
                pool.wait_ge(s_w[w], 16)
                cols = slice(w * WP, (w + 1) * WP)
                pool.tensor_copy(w_hi[:, cols], w_raw[:, w % 2, :]).then_inc(w_hi_done, 1)
                pool.wait_ge(w_hi_done, w + 1)
                pool.tensor_tensor(w_lo[:, cols], w_raw[:, w % 2, :], w_hi[:, cols].bitcast(F32),
                                   ALU.subtract).then_inc(w_lo_done, 1)

            def normalise(b):
                pool.wait_ge(ln2_step, RSQRT_STEPS * (b // 4 + 1))
                if b >= 4:
                    pool.wait_ge(xT_ready, (b - 4) // 2 + 1)
                pool.tensor_scalar(xn2[:, b % 4, :], x1[:, b, :], mv[:, 1, b, 0:1], rstd[:, 1, b:b + 1],
                                   ALU.subtract, ALU.mult).then_inc(xn_done, 1)

            lows(0)
            lows(1)
            pool.wait_ge(lo_q, 2)
            zero_rows(1)
            values(0)
            lows(2)
            pool.wait_ge(lo_q, 3)
            zero_rows(2)
            w = 0
            for b in range(B):
                for _ in range(2):
                    if w < WPARTS:
                        weight(w)
                        w += 1
                if b + 3 < B:
                    lows(b + 3)
                if b + 1 < B:
                    values(b + 1)
                if b >= 1:
                    residual(b - 1)
                if b == 5:
                    for bb in range(4):
                        normalise(bb)
            residual(B - 1)
            for e in range(E):
                last = pool.memset(rev[:, :, e:e + 1], float(E - e))
            last.then_inc(c_rev, 1)
            for c in range(NC):
                pool.wait_ge(r_step, SELECTED * c + SELECTED)
                if c >= 1:
                    pool.wait_ge(mask_ready, 4 * c)
                for i in (2, 3):
                    pool.tensor_scalar(wide_out(i), repeated(i), LORA, None, ALU.mult).then_inc(wide_rest, 1)
                if c == 0:
                    for b in range(4, B):
                        normalise(b)

        @block.scalar
        def _(act):
            def highs(b):
                r = b % 2
                act.wait_ge(s_ctx[min(b // 2, 1)], 16)
                if b >= 2:
                    act.wait_ge(wrote_k[r], 16 * (b // 2))
                    act.wait_ge(wrote_q[r], 16 * (b // 2))
                act.activation(split[:, r, 2, :], c_sb[:, b, :], ACT.Copy).then_inc(hi_k, 1)
                act.wait_ge(qf_ready, b + 1)
                act.activation(split[:, r, 0, :], qf[:, r, :], ACT.Copy).then_inc(hi_q, 1)

            def max_rows(b):
                act.wait_ge(mt_ready, b + 1)
                if b >= 2:
                    act.wait_ge(rows_loaded[b % 2], 16 * (b // 2))
                act.activation(mx_rows[:, b % 2, :], MAX_BANK[0:16, 0:D], ACT.Copy).then_inc(mt_copied, 1)
                act.wait_ge(mt_copied, b + 1)
                if b >= NQ:
                    act.wait_ge(st_ready, H * (b - NQ + 1))
                act.dma_start(Q[MAXROW:MAXROW + 16, b % NQ, :, :].bitcast(F32),
                              mx_rows[:, b % 2, :].bitcast(F32).rearrange("p (a m) -> p a m", a=1).to_broadcast([16, H, D]))\
                    .then_inc(rows_loaded[b % 2], 16)

            def exp(b, i):
                n = H * b + i
                act.wait_ge(st_ready, n + 1)
                if n >= H:
                    act.wait_ge(uz_done, n // 4 - 1)
                act.activation(P[:, n % H, :, :], ST_BANK[n % 2][:, :], ACT.Exp, scale=SCALE).then_inc(exp_done, 1)

            def high_x(p):
                act.wait_ge(xT_ready, p + 1)
                act.activation(pair(xT_hi, p), turned(p), ACT.Copy).then_inc(xT_hi_done, 1)

            highs(0)
            highs(1)
            highs(2)
            act.wait_ge(s_sel, 16)
            for n in range(NQ):
                act.activation(K[MAXROW:MAXROW + 16, n, :, :], sel_sb[MAXROW:MAXROW + 16, :, :], ACT.Copy)\
                    .then_inc(c_sel, 1)
            max_rows(0)
            for b in range(B):
                for i in range(H):
                    exp(b, i)
                    if i == 2 and b >= 6:
                        high_x(b - 6)
                if b + 1 < B:
                    max_rows(b + 1)
                if b + 3 < B:
                    highs(b + 3)

            def copy_logits(c):
                act.wait_ge(lT_ready, c + 1)
                if c >= 1:
                    act.wait_ge(logits_ready, c)
                act.activation(lT[:, :], ROUTE_BANK[c][0:E, :], ACT.Copy).then_inc(lT_copied, 1)

            def copy_z(c, j):
                act.wait_ge(z_ready, 2 * c + j + 1)
                if c >= 1:
                    act.wait_ge(z_masked, 4 * c)
                act.activation(z_raw[:, j, :], ROUTE_BANK[c][:, :], ACT.Copy).then_inc(z_copied, 1)

            def exp_logits(c):
                act.wait_ge(r_step, SELECTED * c + READ)
                if c >= 1:
                    act.wait_ge(r_step, SELECTED * c)
                act.activation(pr[:, :, :], lg[:, :, :], ACT.Exp).then_inc(r_exp, 1)

            def high_z(c, k):
                act.wait_ge(z_masked, 4 * c + k + 1)
                act.activation(z_hi[:, c, k // 2, k % 2, :], z[:, k // 2, k % 2, :], ACT.Copy).then_inc(z_hi_done, 1)

            def copy_mask(c, k):
                act.wait_ge(mask_ready, 4 * c + 2 + k + 1)
                act.activation(weight_mask[:, c, k, :], ROUTE_BANK[c][:, :], ACT.Copy).then_inc(mask_copied, 1)

            def gate(n):
                m, kind = STAGES[n % NS]
                p = TAIL if m == MT - 1 else 128
                act.wait_ge(gu_ready, n + 1)
                if n >= 2:
                    act.wait_ge(hid_done, n - 1)
                act.activation(silu[0:p, n % 2, :], GU_BANK[m % 2][0][0:p, :], ACT.Silu).then_inc(silu_done, 1)

            def high_h(n):
                m, kind = STAGES[n % NS]
                p = TAIL if m == MT - 1 else 128
                act.wait_ge(hid_done, n + 1)
                if n >= 3:
                    act.wait_ge(down_done, n - 2)
                act.activation(h_hi[0:p, n % 3, :], hid[0:p, n % 3, :], ACT.Copy).then_inc(h_hi_done, 1)

            def high_a(c):
                act.wait_ge(low_sum, c + 1)
                if c >= 1:
                    act.wait_ge(o_ready, 2 * c)
                act.activation(a_hi[:, :], low[:, 0, :], ACT.Copy).then_inc(a_hi_done, 1)

            copy_logits(0)
            exp_logits(0)
            copy_z(0, 0)
            copy_z(0, 1)
            gate(0)
            for k in range(4):
                high_z(0, k)
            gate(1)
            copy_mask(0, 0)
            high_h(0)
            copy_mask(0, 1)
            for n in range(2, NC * NS):
                gate(n)
                high_h(n - 1)
                if n in (4, 5):
                    high_x(n - 2)
                if n == 12:
                    copy_logits(1)
                if n == 13:
                    exp_logits(1)
                    copy_z(1, 0)
                if n == 14:
                    copy_z(1, 1)
                if n == 16:
                    high_z(1, 0)
                    high_z(1, 1)
                if n == 17:
                    high_z(1, 2)
                    high_z(1, 3)
                    copy_mask(1, 0)
                    copy_mask(1, 1)
                if n == NS:
                    high_a(0)
            high_h(NC * NS - 1)
            high_a(NC - 1)

        @block.tensor
        def _(pe):
            def scores(b, i):
                n, q, h = H * b + i, b % NQ, ORDER[i]
                if i == 0:
                    if b < NQ:
                        pe.wait_ge(c_qzero, 2 * b + 2)
                    pe.wait_ge(k_loaded[q], 64 * (b // NQ + 1))
                    pe.wait_ge(q_loaded[q], 64 * (b // NQ + 1))
                if n >= 3:
                    pe.wait_ge(max_done, n - 2)
                for mh in range(2):
                    mm = pe.matmul(S_BANK[n % 3][:, mh * D:(mh + 1) * D], Q[0:96, q, h, mh * 128:(mh + 1) * 128],
                                   K[0:96, q, h, :], start=True, stop=True)
                mm.then_inc(s_ready, 1)

            def scoresT(b, i):
                n, q, h = H * b + i, b % NQ, ORDER[i]
                if i == 0:
                    if b < NQ:
                        pe.wait_ge(c_sel, b + 1)
                    pe.wait_ge(rows_loaded[b % 2], 16 * (b // 2 + 1))
                if n >= 2:
                    pe.wait_ge(exp_done, n - 1)
                rows = MAXROW + 16
                for nh in range(2):
                    mm = pe.matmul(ST_BANK[n % 2][:, nh * D:(nh + 1) * D], K[0:rows, q, h, nh * 128:(nh + 1) * 128],
                                   Q[0:rows, q, h, :], start=True, stop=True)
                mm.then_inc(st_ready, 1)

            def max_rows(b):
                pe.wait_ge(mx_lo, b + 1)
                if b >= 1:
                    pe.wait_ge(mt_copied, b)
                if b == 7:
                    pe.wait_ge(xT_hi_done, 1)
                    pe.wait_ge(xT_lo_done, 1)
                for mh in range(2):
                    mm = pe.matmul(MAX_BANK[0:16, mh * 128:(mh + 1) * 128],
                                   mx_split[:, b % 2, mh, :, :].bitcast(F32).rearrange("p a h -> p (a h)"),
                                   ident[:, :], start=True, stop=True)
                mm.then_inc(mt_ready, 1)

            def pv(b, s):
                pe.wait_ge(exp_done, H * b + 4 * (s + 1))
                uz = UZ_BANK[b % 2]
                if s == 0:
                    pe.wait_ge(v_ready, b + 1)
                    if b >= 2:
                        pe.wait_ge(at_done, b - 1)
                for nh in range(2):
                    for p in range(4):
                        pe.matmul(uz[32 * p:32 * p + 32, 0:D], V[:, b % 2, nh, 2 * p + s, :], P[:, 4 * s + p, nh, :],
                                  start=(s == 0 and nh == 0), stop=(s == 1 and nh == 1), skip_group_check=True)
                    for p in range(4):
                        mm = pe.matmul(uz[32 * p:32 * p + 32, D:2 * D], ones[:, s, :], P[:, 4 * s + p, nh, :],
                                       start=False, stop=(s == 1 and nh == 1), skip_group_check=True)
                mm.then_inc(uz_done, 1)

            def turn_x(p):
                pe.wait_ge(xn_done, 2 * p + 2)
                if p < 2:
                    pe.wait_ge(mt_copied, 7 + p)
                if p == 2:
                    pe.wait_ge(max_done, H * B)
                if p == 3:
                    pe.wait_ge(xT_hi_done, p)
                    pe.wait_ge(xT_lo_done, p)
                for b in (2 * p, 2 * p + 1):
                    for k in range(KD):
                        mm = pe.transpose(turned(p)[:, b % 2, k, :], xn2[:, b % 4, k * 128:(k + 1) * 128], ident[:, :])
                mm.then_inc(xT_ready, 1)

            pe.wait_ge(c_ident, 2)
            pe.wait_ge(c_ones, 2)
            for i in range(H):
                scores(0, i)
            max_rows(0)
            for b in range(B):
                more = b + 1 < B
                if more:
                    for i in range(3):
                        scores(b + 1, i)
                if b >= 1:
                    pv(b - 1, 1)
                if b >= 6:
                    turn_x(b - 6)
                for i in range(H):
                    scoresT(b, i)
                    if more and i + 3 < H:
                        scores(b + 1, i + 3)
                    if i == 5:
                        pv(b, 0)
                if more:
                    max_rows(b + 1)
            pv(B - 1, 1)

            xT = (xT_hi, xT_lo)

            def logits(c):
                if c == 0:
                    pe.wait_ge(w_lo_done, WPARTS)
                    pe.wait_ge(xT_hi_done, 2)
                    pe.wait_ge(xT_lo_done, 2)
                else:
                    pe.wait_ge(hid_done, 12)
                    pe.wait_ge(xT_hi_done, 4)
                    pe.wait_ge(xT_lo_done, 4)
                for i, (wp, xp) in enumerate(PASSES):
                    for k in range(KD):
                        mm = pe.matmul(ROUTE_BANK[c][0:E, :], W(wp, "wr", k * E, E), xT[xp][:, k, c * C:(c + 1) * C],
                                       start=(i == 0 and k == 0), stop=(i == 2 and k == KD - 1))
                mm.then_inc(lT_ready, 1)

            def turn_logits(c):
                pe.wait_ge(lT_copied, c + 1)
                for t in range(TC):
                    mm = pe.matmul(ROUTE_BANK[c][:, t * E:(t + 1) * E], lT[:, t * 128:(t + 1) * 128], ident[0:E, 0:E],
                                   start=True, stop=True)
                mm.then_inc(logits_ready, 1)

            def z_rows(c, j):
                if j == 0:
                    pe.wait_ge(r_step, SELECTED * c + READ)
                else:
                    pe.wait_ge(z_copied, 2 * c + 1)
                for i, (wp, xp) in enumerate(PASSES):
                    for k in range(KD):
                        mm = pe.matmul(ROUTE_BANK[c][:, :], W(wp, ("ag", "au")[j], k * 128, 128),
                                       xT[xp][:, k, c * C:(c + 1) * C], start=(i == 0 and k == 0),
                                       stop=(i == 2 and k == KD - 1))
                mm.then_inc(z_ready, 1)

            def masks(c, i):
                if i == 0:
                    pe.wait_ge(z_copied, 2 * c + 2)
                if i in (1, 2):
                    pe.wait_ge(z_masked, 4 * c + 2 * i)
                if i == 3:
                    pe.wait_ge(mask_copied, 2 * c + 1)
                if i < 2:
                    pe.wait_ge(wide_first, 2 * c + i + 1)
                else:
                    pe.wait_ge(wide_rest, 2 * c + i - 1)
                for t in range(TC):
                    mm = pe.transpose(ROUTE_BANK[c][:, t * 128:(t + 1) * 128],
                                      wide[:, i, t, :, :].rearrange("p e r -> p (e r)"), ident[:, :])
                mm.then_inc(mask_ready, 1)

            def stage(c, i):
                m, kind = STAGES[i]
                n = NS * c + i
                g, u = GU_BANK[m % 2]
                if n < 2:
                    if n == 0:
                        pe.wait_ge(max_done, H * B)
                    else:
                        pe.wait_ge(exp_done, H * B)
                else:
                    pe.wait_ge(hid_done, n - 1)
                if c >= 1 and i == 1:
                    pe.wait_ge(mask_copied, 2 * c + 2)
                if i == 2:
                    pe.wait_ge(z_hi_done, 4 * c + 2)
                    pe.wait_ge(z_lo_done, 4 * c + 2)
                if i == 4:
                    pe.wait_ge(z_hi_done, 4 * c + 4)
                    pe.wait_ge(z_lo_done, 4 * c + 4)
                tail = m == MT - 1
                if kind == 0:
                    for wp, xp in PASSES:
                        for k in range(KD):
                            rhs = xT[xp][:, k, c * C:(c + 1) * C]
                            first = (wp, xp, k) == (0, 0, 0)
                            mm = pe.matmul(g[:, :], W(wp, "wg", (k * MT + m) * 128, 128), rhs,
                                           start=first, stop=False, skip_group_check=True)
                            if not tail:
                                mm = pe.matmul(u[:, :], W(wp, "wu", (k * (MT - 1) + m) * 128, 128), rhs,
                                               start=first, stop=False, skip_group_check=True)
                else:
                    for j, (name, to) in enumerate((("bg", g), ("bu", g if tail else u))):
                        for wp, zp in PASSES:
                            mm = pe.matmul(to[:, :], W(wp, name, m * 128, 128), (z_hi, z_lo)[zp][:, c, kind - 1, j, :],
                                           start=False, stop=(kind == 2), skip_group_check=True)
                mm.then_inc(gu_ready, 1)

            def down(c, i):
                m, kind = STAGES[i]
                n = NS * c + i
                s = n % 3
                pe.wait_ge(h_hi_done, n + 1)
                pe.wait_ge(h_lo_done, n + 1)
                if i == 0:
                    if c == 0:
                        pe.wait_ge(mask_copied, 2)
                        pe.wait_ge(at_done, B)
                    else:
                        pe.wait_ge(y_done, 2 * c)
                if c == 0 and (m, kind) == (0, 2):
                    pe.wait_ge(xT_hi_done, 4)
                    pe.wait_ge(xT_lo_done, 4)
                if c >= 1 and m == 0 and kind > 0:
                    pe.wait_ge(low_done, 2 * (c - 1) + kind)
                passes = [(0, h_hi), (1, h_hi)] if m == MT - 1 else [(0, h_hi), (1, h_hi), (0, h_lo)]
                for j, (wp, h) in enumerate(passes):
                    if kind == 0:
                        for t in range(TC):
                            mm = pe.matmul(O_BANK[t // 2][:, (t % 2) * D:(t % 2 + 1) * D],
                                           h[:, s, t * 128:(t + 1) * 128], W(wp, "wd", m * D, D),
                                           start=(m == 0 and j == 0 and t % 2 == 0), stop=False, skip_group_check=True)
                    else:
                        mm = pe.matmul(D_BANK[kind - 1][:, :], W(wp, "ad", m * 128, 128), h[:, s, :],
                                       start=(m == 0 and j == 0), stop=(m == MT - 1 and j == len(passes) - 1))
                mm.then_inc(down_done, 1)

            def lora_out(c):
                pe.wait_ge(a_hi_done, c + 1)
                pe.wait_ge(a_lo_done, c + 1)
                for o in range(2):
                    for t in (2 * o, 2 * o + 1):
                        for wp, a in ((0, a_hi), (1, a_hi), (0, a_lo)):
                            mm = pe.matmul(O_BANK[o][:, (t % 2) * D:(t % 2 + 1) * D], a[:, t * 128:(t + 1) * 128],
                                           W(wp, "bd", 0, D), start=False, stop=True, skip_group_check=True)
                    mm.then_inc(o_ready, 1)

            logits(0)
            stage(0, 0)
            turn_logits(0)
            z_rows(0, 0)
            z_rows(0, 1)
            stage(0, 1)
            for i in range(4):
                masks(0, i)
            for c in range(NC):
                for i in range(2, NS):
                    stage(c, i)
                    if c == 0 and i in (4, 5):
                        turn_x(i - 2)
                    if c == 0 and i == 12:
                        logits(1)
                    if c == 0 and i == 13:
                        turn_logits(1)
                    if c == 0 and i == 14:
                        z_rows(1, 1)
                    if c == 0 and i == 16:
                        masks(1, 1)
                    if c == 0 and i == 17:
                        masks(1, 3)
                    down(c, i - 2)
                    if c == 0 and i == 13:
                        z_rows(1, 0)
                    if c == 0 and i == 15:
                        masks(1, 0)
                    if c == 0 and i == 16:
                        masks(1, 2)
                if c + 1 < NC:
                    stage(c + 1, 0)
                down(c, NS - 2)
                down(c, NS - 1)
                if c + 1 < NC:
                    stage(c + 1, 1)
                lora_out(c)

        @block.vector
        def _(dve):
            def low_x(p):
                dve.wait_ge(xT_hi_done, p + 1)
                dve.tensor_tensor(pair(xT_lo, p), turned(p), pair(xT_hi, p).bitcast(F32), ALU.subtract)\
                    .then_inc(xT_lo_done, 1)

            def rsqrt(which, b0, b1, done, at_least):
                cols = slice(b0, b1)
                v, t, y = nr_v[:, cols], nr_t[:, cols], rstd[:, which, cols]
                steps = [lambda: dve.tensor_scalar(v, mv[:, which, cols, 1], EPS, None, ALU.add),
                         lambda: dve.tensor_scalar(y.bitcast(U32), v.bitcast(U32), 1, None, ALU.logical_shift_right),
                         lambda: dve.tensor_scalar(y.bitcast(I32), y.bitcast(I32), -1, RSQRT_SEED, ALU.mult, ALU.add)]
                for _ in range(3):
                    steps += [lambda: dve.scalar_tensor_tensor(out=t, in0=y, scalar=-0.5, in1=y, op0=ALU.mult, op1=ALU.mult),
                              lambda: dve.tensor_tensor(t, t, v, ALU.mult),
                              lambda: dve.scalar_tensor_tensor(out=y, in0=t, scalar=1.5, in1=y, op0=ALU.add, op1=ALU.mult)]
                assert len(steps) == RSQRT_STEPS
                for n, step in enumerate(steps):
                    step().then_inc(done, 1)
                    dve.wait_ge(done, at_least + n + 1)
                return at_least + len(steps)

            def ln1_stats(b):
                dve.wait_ge(s_x[b], 16)
                dve.bn_stats(stats[:, 0, b, :], x_sb[:, b, :]).then_inc(ln_stat, 1)
                dve.wait_ge(ln_stat, 2 * b + 1)
                dve.bn_aggr(mv[:, 0, b, :], stats[:, 0, b, :]).then_inc(ln_stat, 1)

            def q_full(b):
                if b >= 2:
                    dve.wait_ge(lo_q, b - 1)
                dve.tensor_scalar(qf[:, b % 2, :], x_sb[:, b, :], mv[:, 0, b, 0:1], rstd[:, 0, b:b + 1],
                                  ALU.subtract, ALU.mult).then_inc(qf_ready, 1)

            def maxima(b, i):
                n = H * b + i
                dve.wait_ge(s_ready, n + 1)
                if i == 0 and b >= 2:
                    dve.wait_ge(mx_lo, b - 1)
                dve.tensor_reduce(mx[:, b % 2, :, ORDER[i]], S_BANK[n % 3][:, :].rearrange("p (a n) -> p a n", a=2),
                                  AX.X, ALU.max).then_inc(max_done, 1)

            def max_split(b):
                r = b % 2
                dve.wait_ge(max_done, H * (b + 1))
                if b >= 2:
                    dve.wait_ge(mt_ready, b - 1)
                dve.tensor_copy(mx_split[:, r, :, 0, :], mx[:, r, :, :]).then_inc(mx_hi, 1)
                dve.wait_ge(mx_hi, b + 1)
                dve.tensor_tensor(mx_split[:, r, :, 1, :], mx[:, r, :, :], mx_split[:, r, :, 0, :].bitcast(F32),
                                  ALU.subtract).then_inc(mx_lo, 1)

            def norm(b):
                dve.wait_ge(uz_done, 2 * (b + 1))
                dve.reciprocal(rz[:, :], UZ_BANK[b % 2][:, D:2 * D]).then_inc(rz_done, 1)
                dve.wait_ge(rz_done, b + 1)
                if b >= 2:
                    dve.wait_ge(x1_done, b - 1)
                dve.tensor_tensor(at[:, b % 2, :], UZ_BANK[b % 2][:, 0:D], rz[:, :], ALU.mult).then_inc(at_done, 1)

            def ln2_stats(b):
                dve.wait_ge(x1_done, b + 1)
                dve.bn_stats(stats[:, 1, b, :], x1[:, b, :]).then_inc(ln2_stat, 1)
                dve.wait_ge(ln2_stat, 2 * b + 1)
                dve.bn_aggr(mv[:, 1, b, :], stats[:, 1, b, :]).then_inc(ln2_stat, 1)

            ln1_stats(0)
            ln1_stats(1)
            dve.wait_ge(ln_stat, 4)
            at_step = rsqrt(0, 0, 2, ln_step, 0)
            q_full(0)
            q_full(1)
            for b in range(2, B):
                ln1_stats(b)
            dve.wait_ge(ln_stat, 2 * B)
            rsqrt(0, 2, B, ln_step, at_step)
            q_full(2)
            for i in range(H):
                maxima(0, i)
            max_split(0)
            for b in range(B):
                if b + 1 < B:
                    for i in range(H):
                        maxima(b + 1, i)
                        if i == 4 and b == 6:
                            low_x(0)
                    max_split(b + 1)
                else:
                    low_x(1)
                if b >= 1:
                    norm(b - 1)
                if b + 3 < B:
                    q_full(b + 3)
                if b >= 2:
                    ln2_stats(b - 2)
                if b == 5:
                    dve.wait_ge(ln2_stat, 8)
                    rsqrt(1, 0, 4, ln2_step, 0)
            norm(B - 1)

            step = [0]

            def done(ins):
                step[0] += 1
                ins.then_inc(r_step, 1)
                dve.wait_ge(r_step, step[0])

            def col(i):
                return mcol[:, i, :].rearrange("p (t a) -> p t a", a=1).to_broadcast([128, TC, E])

            def choose(c):
                dve.wait_ge(logits_ready, c + 1)
                if c == 0:
                    dve.wait_ge(c_rev, 1)
                else:
                    dve.wait_ge(wide_rest, 2 * c)
                    dve.wait_ge(r_exp, c)
                lgt = ROUTE_BANK[c][:, 0:TC * E].rearrange("p (t e) -> p t e", e=E)
                done(dve.tensor_reduce(mcol[:, 0, :], lgt, AX.X, ALU.max))
                done(dve.tensor_tensor(lg[:, :, :], lgt, col(0), ALU.subtract))
                assert step[0] == SELECTED * c + READ
                done(dve.scalar_tensor_tensor(out=tmp[:, :, :], in0=lg[:, :, :], scalar=0.0, in1=rev[:, :, :],
                                              op0=ALU.is_ge, op1=ALU.mult))
                done(dve.tensor_reduce(mcol[:, 1, :], tmp[:, :, :], AX.X, ALU.max))
                done(dve.tensor_tensor(sels[:, 0, :, :], rev[:, :, :], col(1), ALU.is_equal))
                done(dve.scalar_tensor_tensor(out=lg2[:, :, :], in0=sels[:, 0, :, :], scalar=-3e38, in1=lg[:, :, :],
                                              op0=ALU.mult, op1=ALU.add))
                done(dve.tensor_reduce(mcol[:, 2, :], lg2[:, :, :], AX.X, ALU.max))
                done(dve.tensor_tensor(tmp[:, :, :], lg2[:, :, :], col(2), ALU.is_ge))
                done(dve.tensor_tensor(tmp[:, :, :], tmp[:, :, :], rev[:, :, :], ALU.mult))
                done(dve.tensor_reduce(mcol[:, 3, :], tmp[:, :, :], AX.X, ALU.max))
                done(dve.tensor_tensor(second[:, :, :], rev[:, :, :], col(3), ALU.is_equal))
                done(dve.tensor_tensor(sels[:, 1, :, :], second[:, :, :], sels[:, 0, :, :], ALU.subtract))
                assert step[0] == SELECTED * c + CHOSEN
                if c >= 1:
                    dve.wait_ge(mask_ready, 4 * c)
                for i in range(2):
                    dve.tensor_scalar(wide_out(i), repeated(i), LORA, None, ALU.mult).then_inc(wide_first, 1)

            def weigh(c):
                dve.wait_ge(r_exp, c + 1)
                done(dve.tensor_reduce(mcol[:, 4, :], pr[:, :, :], AX.X, ALU.add))
                done(dve.reciprocal(mcol[:, 5, :], mcol[:, 4, :]))
                done(dve.tensor_tensor(pr[:, :, :], pr[:, :, :], col(5), ALU.mult))
                done(dve.tensor_tensor(sels[:, 2, :, :], pr[:, :, :], sels[:, 0, :, :], ALU.mult))
                done(dve.tensor_tensor(sels[:, 3, :, :], pr[:, :, :], second[:, :, :], ALU.mult))
                done(dve.tensor_copy(mcol[:, 0, :], mcol[:, 5, :]))
                assert step[0] == SELECTED * (c + 1)

            def mask_z(c, d):
                dve.wait_ge(mask_ready, 4 * c + d + 1)
                dve.wait_ge(z_copied, 2 * c + 2)
                if c >= 1:
                    dve.wait_ge(z_hi_done, 4 * c)
                    dve.wait_ge(z_lo_done, 4 * c)
                for j in range(2):
                    dve.tensor_tensor(z[:, d, j, :], z_raw[:, j, :], ROUTE_BANK[c][:, :], ALU.mult).then_inc(z_masked, 1)

            def low_z(c, d):
                for j in range(2):
                    dve.wait_ge(z_hi_done, 4 * c + 2 * d + j + 1)
                    dve.tensor_tensor(z_lo[:, c, d, j, :], z[:, d, j, :], z_hi[:, c, d, j, :].bitcast(F32),
                                      ALU.subtract).then_inc(z_lo_done, 1)

            def gate(n):
                m, kind = STAGES[n % NS]
                tail = m == MT - 1
                p = TAIL if tail else 128
                dve.wait_ge(silu_done, n + 1)
                if n >= 3:
                    dve.wait_ge(h_hi_done, n - 2)
                    dve.wait_ge(h_lo_done, n - 2)
                up = GU_BANK[m % 2][0][64:128, :] if tail else GU_BANK[m % 2][1][:, :]
                dve.tensor_tensor(hid[0:p, n % 3, :], silu[0:p, n % 2, :], up, ALU.mult).then_inc(hid_done, 1)

            def low_h(n):
                m, kind = STAGES[n % NS]
                tail = m == MT - 1
                p = TAIL if tail else 128
                dve.wait_ge(h_hi_done, n + 1)
                dve.wait_ge(hid_done, n + 1)
                to = h_hi[64:128, n % 3, :] if tail else h_lo[:, n % 3, :]
                dve.tensor_tensor(to, hid[0:p, n % 3, :], h_hi[0:p, n % 3, :].bitcast(F32),
                                  ALU.subtract).then_inc(h_lo_done, 1)

            def down_rows(c):
                dve.wait_ge(down_done, NS * (c + 1))
                dve.wait_ge(mask_copied, 2 * c + 2)
                if c >= 1:
                    dve.wait_ge(a_hi_done, c)
                for k in range(2):
                    dve.tensor_tensor(low[:, k, :], D_BANK[k][:, :], weight_mask[:, c, k, :], ALU.mult)\
                        .then_inc(low_done, 1)
                dve.wait_ge(low_done, 2 * c + 2)
                dve.tensor_tensor(low[:, 0, :], low[:, 0, :], low[:, 1, :], ALU.add).then_inc(low_sum, 1)

            def finish(c):
                dve.wait_ge(a_hi_done, c + 1)
                if c >= 1:
                    dve.wait_ge(o_ready, 2 * c)
                dve.tensor_tensor(a_lo[:, :], low[:, 0, :], a_hi[:, :].bitcast(F32), ALU.subtract).then_inc(a_lo_done, 1)
                for o in range(2):
                    n = 2 * c + o
                    dve.wait_ge(o_ready, n + 1)
                    if c >= 1:
                        dve.wait_ge(s_out[o], 16 * c)
                    b = TC * c + 2 * o
                    dve.tensor_tensor(y_sb[:, o, :], x1[:, b:b + 2, :].rearrange("p b d -> p (b d)"), O_BANK[o][:, :],
                                      ALU.add).then_inc(y_done, 1)

            choose(0)
            mask_z(0, 0)
            low_z(0, 0)
            mask_z(0, 1)
            weigh(0)
            gate(0)
            low_z(0, 1)
            gate(1)
            low_h(0)
            ln2_stats(B - 2)
            ln2_stats(B - 1)
            dve.wait_ge(ln2_stat, 2 * B)
            rsqrt(1, 4, B, ln2_step, RSQRT_STEPS)
            for n in range(2, NC * NS):
                gate(n)
                low_h(n - 1)
                if n in (4, 5):
                    low_x(n - 2)
                if n == 13:
                    choose(1)
                if n == 14:
                    weigh(1)
                if n == 15:
                    mask_z(1, 0)
                if n == 16:
                    low_z(1, 0)
                    mask_z(1, 1)
                if n == 17:
                    low_z(1, 1)
                if n == NS:
                    down_rows(0)
                if n == NS + 1:
                    finish(0)
            low_h(NC * NS - 1)
            down_rows(NC - 1)
            finish(NC - 1)


_OUTS = [((8, 128, 256), "float32")]


def kernel(**inputs):
    import numpy as _np
    import concourse.bacc as _bacc
    from concourse import mybir as _mybir
    from concourse.bass_utils import run_bass_kernel_spmd as _run

    a = {k: _np.ascontiguousarray(v) for k, v in inputs.items()}
    ctx_in = a["ctx_2048"]

    def tiles(m, width):
        k = m.shape[0] // 128
        o = _np.zeros((128, k, width), m.dtype)
        o[:, :, :m.shape[1]] = m.reshape(k, 128, m.shape[1]).transpose(1, 0, 2)
        return o.reshape(128, k * width)

    full, tail = (MT - 1) * 128, TAIL
    wg, wu = a["L0_ffn_Wg"].T, a["L0_ffn_Wu"].T
    wg_l = _np.concatenate([wg, wu[:, full:]], axis=1)
    wu_l = wu[:, :full]
    ag = a["L0_ffn_Ag"].reshape(E * RANK, D).T
    au = a["L0_ffn_Au"].reshape(E * RANK, D).T
    bg = a["L0_ffn_Bg"].transpose(0, 2, 1).reshape(E * RANK, F)
    bu = a["L0_ffn_Bu"].transpose(0, 2, 1).reshape(E * RANK, F)
    pad = _np.zeros((E * RANK, tail), bg.dtype)
    bg_l = _np.concatenate([bg, pad], axis=1)
    bu_l = _np.concatenate([bu[:, :full], pad, bu[:, full:]], axis=1)

    def twice_tail(m):
        return tiles(_np.concatenate([m, m[full:]], axis=0), m.shape[1])

    wd_l = twice_tail(a["L0_ffn_Wd"].T)
    ad_l = twice_tail(a["L0_ffn_Ad"].reshape(E * RANK, F).T)
    bd_l = a["L0_ffn_Bd"].transpose(0, 2, 1).reshape(E * RANK, D)
    parts = {"wg": tiles(wg_l, MT * 128), "wu": tiles(wu_l, (MT - 1) * 128), "ag": tiles(ag, 128), "au": tiles(au, 128),
             "wr": tiles(a["L0_ffn_Wr"].T, E), "bg": bg_l, "bu": bu_l, "wd": wd_l, "ad": ad_l, "bd": bd_l}
    weights = _np.concatenate([parts[name] for name, _ in PIECES], axis=1)
    sel = _np.zeros((2, H, H, D), _np.float32)
    for h in range(H):
        sel[:, h, h, :] = -1.0
    arrays = {
        "x": a["x"], "ctx_in": ctx_in, "ctxT": _np.ascontiguousarray(ctx_in.transpose(0, 2, 1)),
        "weights": _np.ascontiguousarray(weights), "sel": sel.reshape(2 * H, H, D),
    }
    nc = _bacc.Bacc("TRN2", target_bir_lowering=False, num_devices=1)
    args = [nc.dram_tensor(n, v.shape, _mybir.dt.from_np(v.dtype), kind="ExternalInput").ap() for n, v in arrays.items()]
    for i, (shape, dtype) in enumerate(_OUTS):
        args.append(nc.dram_tensor(f"out_{i}", shape, _mybir.dt.from_np(_np.dtype(dtype)), kind="ExternalOutput").ap())
    xattn_lora_ffn_kernel(nc, *args)
    r = _run(nc, [arrays], core_ids=[0])
    return r.results[0]["out_0"]
```

```python
from contextlib import ExitStack

import concourse.bass as bass
from concourse import mybir

F32 = mybir.dt.float32
F32R = mybir.dt.float32r
I32 = mybir.dt.int32
U32 = mybir.dt.uint32
ALU = mybir.AluOpType
ACT = mybir.ActivationFunctionType
AX = mybir.AxisListType

B, R, D = 8, 128, 256
H, HD = 8, 16
SCALE = float(HD) ** -0.5
F = 704
E, RANK = 8, 16
LORA = 2.0
EPS = 1e-5
NT = B * R
KD = D // 128
MT = (F + 127) // 128
TAIL = F - (MT - 1) * 128
C = 512
NC = NT // C
TC = C // 128
ORDER = [0, 2, 4, 6, 1, 3, 5, 7]
NQ = 3
NH = 6
LAG = 3
MAXROW = 96
RSQRT_SEED = 0x5F3759DF
RSQRT_STEPS = 12

PIECES = [("wr", KD * E), ("ag", KD * 128), ("au", KD * 128), ("wg", KD * MT * 128), ("wu", KD * (MT - 1) * 128),
          ("bg", MT * 128), ("bu", MT * 128), ("wd", MT * D), ("ad", MT * 128), ("bd", D)]
AT = {}
NW = 0
for _name, _n in PIECES:
    AT[_name] = NW
    NW += _n
WPARTS = 8
WP = NW // WPARTS
STACK_Q, STACK_K = (0, 0, 1), (0, 1, 0)


def parts_to(name):
    return -(-(AT[name] + dict(PIECES)[name]) // WP)


def xattn_lora_ffn_kernel(nc, x, ctx_in, ctxT, weights, sel, out):
    xv = x.rearrange("b r d -> r b d")
    cv = ctx_in.rearrange("b r d -> r b d")
    tv = ctxT.rearrange("b (k p) r -> p b k r", p=128)
    ov = out.rearrange("b r d -> r b d")
    scratch = nc.dram_tensor("scratch", [B, 4, R, D], F32, kind="Internal").ap()

    with ExitStack() as ctx:
        def sb(name, shape, dt=F32, to=None):
            return (to or ctx).enter_context(nc.sbuf_tensor(name, shape, dt))

        def sem(name):
            return ctx.enter_context(nc.semaphore(name))

        bank = [ctx.enter_context(nc.psum_tensor(f"bank{i}", [128, 512], F32)) for i in range(8)]
        S_BANK, ST_BANK, MAX_BANK, UZ_BANK = [bank[0], bank[1], bank[7]], bank[2:4], bank[4], bank[5:7]
        GU_BANK, O_BANK, D_BANK = [bank[0:2], bank[2:4]], bank[4:6], bank[6:8]
        LOGIT_BANK = [bank[4], bank[7]]
        Z_BANK = [[bank[0], bank[1]], [bank[3], bank[3]]]
        MASK_BANK = [[bank[4], bank[7], bank[4], bank[7]], [bank[3]] * 4]

        x_sb = sb("x_sb", [128, B, D])
        x1 = sb("x1", [128, B, D])
        w_hi = sb("w_hi", [128, NW], F32R)
        w_lo = sb("w_lo", [128, NW], F32R)
        w_raw = sb("w_raw", [128, 2, WP])
        ident = sb("ident", [128, 128])
        stats = sb("stats", [128, 2, B, 6])
        mv = sb("mv", [128, 2, B, 2])
        rstd = sb("rstd", [128, 2, B])
        nr_v = sb("nr_v", [128, B])
        nr_t = sb("nr_t", [128, B])
        xT_hi = sb("xT_hi", [128, KD, NT], F32R)
        xT_lo = sb("xT_lo", [128, KD, NT], F32R)
        xn2 = sb("xn2", [128, 4, D])

        sel_sb = x1
        att = ExitStack()
        c_sb = sb("c_sb", [128, B, D], to=att)
        ct_sb = sb("ct_sb", [128, B, 2, R], to=att)
        qf = sb("qf", [128, 2, D], to=att)
        split = sb("split", [128, 2, 4, D], F32R, to=att)
        Q = sb("Q", [128, NQ, H, D], F32R, to=att)
        K = sb("K", [128, NQ, H, D], F32R, to=att)
        V = sb("V", [128, 2, 2, H, 32], to=att)
        ones = sb("ones", [128, 2, 32], to=att)
        P = sb("P", [128, H, 2, D], to=att)
        mx = sb("mx", [128, 2, 2, H], to=att)
        mx_split = sb("mx_split", [128, 2, 2, 2, H], F32R, to=att)
        mx_rows = sb("mx_rows", [16, 2, D], F32R, to=att)
        rz = sb("rz", [128, D], to=att)
        at = sb("at", [128, 2, D], to=att)
        att.close()
        z_raw = sb("z_raw", [128, 2, C])
        lT = sb("lT", [E, C])
        rev = sb("rev", [128, TC, E])
        lg = sb("lg", [128, TC, E])
        lg2 = sb("lg2", [128, TC, E])
        pr = sb("pr", [128, TC, E])
        tmp = sb("tmp", [128, TC, E])
        mcol = sb("mcol", [128, 6, TC])
        sels = sb("sels", [128, 4, TC, E])
        second = sb("second", [128, TC, E])
        z = sb("z", [128, 2, 2, C])
        wide = sb("wide", [128, 4, TC, E, RANK])
        z_hi = sb("z_hi", [128, NC, 2, 2, C], F32R)
        z_lo = sb("z_lo", [128, NC, 2, 2, C], F32R)
        weight_mask = sb("weight_mask", [128, NC, 2, C])
        silu = sb("silu", [128, 2, C])
        hid = sb("hid", [128, 3, C])
        h_hi = sb("h_hi", [128, NH, C], F32R)
        h_lo = sb("h_lo", [128, NH, C], F32R)
        low = sb("low", [128, 2, C])
        a_hi = sb("a_hi", [128, C], F32R)
        a_lo = xT_lo[:, 0, 0:C]
        y_sb = xn2.rearrange("p (o b) d -> p o (b d)", o=2)

        s_x = [sem(f"s_x{i}") for i in range(4)]
        s_ctx = [sem(f"s_ctx{i}") for i in range(4)]
        s_ctxT = [sem(f"s_ctxT{i}") for i in range(2)]
        s_sel = [sem(f"s_sel{i}") for i in range(NQ)]
        s_w = [sem(f"s_w{i}") for i in range(WPARTS)]
        c_ident = sem("c_ident")
        c_ones = sem("c_ones")
        c_vzero = sem("c_vzero")
        c_zero0k = sem("c_zero0k")
        c_zero0q = sem("c_zero0q")
        c_zero = sem("c_zero")
        c_sel = sem("c_sel")
        c_rev = sem("c_rev")
        ln_stat = sem("ln_stat")
        ln_step = sem("ln_step")
        qf_ready = sem("qf_ready")
        hi_q = sem("hi_q")
        hi_k = sem("hi_k")
        lo_q = sem("lo_q")
        lo_k = sem("lo_k")
        v_ready = sem("v_ready")
        wrote_q = [sem(f"wrote_q{i}") for i in range(2)]
        wrote_k = [sem(f"wrote_k{i}") for i in range(2)]
        q_loaded = [sem(f"q_loaded{i}") for i in range(NQ)]
        k_loaded = [sem(f"k_loaded{i}") for i in range(NQ)]
        s_ready = sem("s_ready")
        max_done = sem("max_done")
        mx_hi = sem("mx_hi")
        mx_lo = sem("mx_lo")
        mt_ready = sem("mt_ready")
        mt_copied = sem("mt_copied")
        rows_loaded = [sem(f"rows_loaded{i}") for i in range(2)]
        st_ready = sem("st_ready")
        exp_done = sem("exp_done")
        uz_done = sem("uz_done")
        rz_done = sem("rz_done")
        at_done = sem("at_done")
        x1_done = sem("x1_done")
        w_hi_done = sem("w_hi_done")
        w_lo_done = sem("w_lo_done")
        ln2_stat = sem("ln2_stat")
        ln2_step = sem("ln2_step")
        xn_done = sem("xn_done")
        xT_ready = sem("xT_ready")
        xT_hi_done = sem("xT_hi_done")
        xT_lo_done = sem("xT_lo_done")
        lT_ready = sem("lT_ready")
        lT_copied = sem("lT_copied")
        logits_ready = sem("logits_ready")
        r_step = sem("r_step")
        r_exp = sem("r_exp")
        wide_first = sem("wide_first")
        wide_rest = sem("wide_rest")
        mask_ready = sem("mask_ready")
        mask_copied = sem("mask_copied")
        z_ready = sem("z_ready")
        z_copied = sem("z_copied")
        z_masked = sem("z_masked")
        z_hi_done = sem("z_hi_done")
        z_lo_done = sem("z_lo_done")
        gu_ready = sem("gu_ready")
        silu_done = sem("silu_done")
        hid_done = sem("hid_done")
        h_hi_done = sem("h_hi_done")
        h_lo_done = sem("h_lo_done")
        down_done = sem("down_done")
        low_done = sem("low_done")
        low_sum = sem("low_sum")
        a_hi_done = sem("a_hi_done")
        a_lo_done = sem("a_lo_done")
        o_ready = sem("o_ready")
        y_done = sem("y_done")
        s_out = [sem(f"s_out{i}") for i in range(2)]

        block = ctx.enter_context(nc.Block())

        def W(part, name, at_col, n):
            a = AT[name] + at_col
            return (w_hi, w_lo)[part][:, a:a + n]

        PASSES = [(0, 0), (1, 0), (0, 1)]

        STAGES = [(m, kind) for m0 in range(0, MT, 2) for kind in range(3) for m in (m0, m0 + 1)]
        NS = len(STAGES)

        def spans(n):
            return [slice(0, C)] if n < NC * NS - 1 else [slice(0, C // 2), slice(C // 2, C)]

        LAST_DOWNS = [NS - 4, NS - 3, NS - 6, NS - 2, NS - 1, NS - 5]

        READ, CHOSEN, SELECTED = 2, 12, 18

        def group(b):
            return min(b, 2) if b < 4 else 3

        def repeated(i):
            return sels[:, i, :, :].rearrange("p t (e a) -> p (t e) a", a=1).to_broadcast([128, TC * E, RANK])

        def wide_out(i):
            return wide[:, i, :, :, :].rearrange("p t e r -> p (t e) r")

        def pair(xT, p):
            return xT[:, :, 256 * p:256 * (p + 1)].rearrange("p k (b t) -> p b k t", b=2)

        def turned(p):
            bk = MAX_BANK if p == 0 else bank[7]
            return bk[:, :].rearrange("p (b k t) -> p b k t", b=2, k=KD)

        @block.sync
        def _(sp):
            def load(dst, src, g, done):
                b0, b1 = ((0, 1), (1, 2), (2, 4), (4, B))[g]
                sp.dma_start(dst[:, b0:b1, :], src[:, b0:b1, :]).then_inc(done[g], 16)

            def write_k(b):
                sp.wait_ge(lo_k, b + 1)
                sp.dma_start(scratch[b, 2:4].rearrange("t p m -> p t m"), split[:, b % 2, 2:4, :].bitcast(F32))\
                    .then_inc(wrote_k[b % 2], 16)

            def write_q(b):
                sp.wait_ge(lo_q, b + 1)
                sp.dma_start(scratch[b, 0:2].rearrange("t p m -> p t m"), split[:, b % 2, 0:2, :].bitcast(F32))\
                    .then_inc(wrote_q[b % 2], 16)

            def stacks(b, buf, half0, halves, wrote, loaded):
                n = b % NQ
                if b >= NQ:
                    sp.wait_ge(st_ready, H * (b - NQ + 1))
                elif b == 0:
                    sp.wait_ge(c_zero0k if buf is K else c_zero0q, 1)
                else:
                    sp.wait_ge(c_zero, 2 * b)
                sp.wait_ge(wrote[b % 2], 16 * (b // 2 + 1))
                for i, half in enumerate(halves):
                    sp.dma_start(buf[HD * i:HD * (i + 1), n, :, :].bitcast(F32),
                                 scratch[b, half0 + half].rearrange("(h d) m -> d h m", d=HD)).then_inc(loaded[n], 16)

            def stack_k(b):
                stacks(b, K, 2, STACK_K, wrote_k, k_loaded)
                if 0 < b < NQ:
                    sp.wait_ge(c_sel, 1)
                    sp.dma_start(K[MAXROW:MAXROW + 16, b, :, :].bitcast(F32), K[MAXROW:MAXROW + 16, 0, :, :].bitcast(F32))\
                        .then_inc(s_sel[b], 16)

            def stack_q(b):
                stacks(b, Q, 0, STACK_Q, wrote_q, q_loaded)

            def load_weights(w):
                if w >= 2:
                    sp.wait_ge(w_lo_done, w - 1)
                sp.dma_start(w_raw[:, w % 2, :], weights[:, w * WP:(w + 1) * WP]).then_inc(s_w[w], 16)

            load(x_sb, xv, 0, s_x)
            load(c_sb, cv, 0, s_ctx)
            load(x_sb, xv, 1, s_x)
            load(c_sb, cv, 1, s_ctx)
            load(x_sb, xv, 2, s_x)
            sp.dma_start(sel_sb[MAXROW:MAXROW + 16, :, :], sel).then_inc(s_sel[0], 16)
            load(c_sb, cv, 2, s_ctx)
            load(x_sb, xv, 3, s_x)
            write_k(0)
            write_k(1)
            write_q(0)
            stack_k(0)
            stack_q(0)
            sp.dma_start(ct_sb[:, 0:2, :, :], tv[:, 0:2, :, :]).then_inc(s_ctxT[0], 16)
            write_q(1)
            write_k(2)
            stack_k(1)
            stack_q(1)
            write_q(2)
            stack_k(2)
            stack_q(2)
            load(c_sb, cv, 3, s_ctx)
            sp.wait_ge(rows_loaded[0], 16)
            sp.dma_start(ct_sb[:, 2:B, :, :], tv[:, 2:B, :, :]).then_inc(s_ctxT[1], 16)
            load_weights(0)
            for b in range(B - 1):
                if b + NQ < B:
                    write_k(b + NQ)
                    write_q(b + NQ)
                    stack_k(b + NQ)
                    stack_q(b + NQ)
                load_weights(b + 1)
            for c in range(NC):
                for o in range(2):
                    n = 2 * c + o
                    sp.wait_ge(y_done, n + 1)
                    sp.dma_start(ov[:, TC * c + 2 * o:TC * c + 2 * o + 2, :],
                                 y_sb[:, n % 2, :].rearrange("p (t d) -> p t d", d=D)).then_inc(s_out[n % 2], 16)
            sp.wait_ge(s_out[0], 16 * NC)
            sp.wait_ge(s_out[1], 16 * NC)

        @block.gpsimd
        def _(pool):
            def zero(buf, n, done):
                pool.memset(buf[:, n, :, :].bitcast(U32), 0).then_inc(done, 1)

            def low_k(b):
                if b >= 2:
                    pool.wait_ge(wrote_k[b % 2], 16 * (b // 2))
                pool.wait_ge(hi_k, b + 1)
                pool.tensor_tensor(split[:, b % 2, 3, :], c_sb[:, b, :], split[:, b % 2, 2, :].bitcast(F32),
                                   ALU.subtract).then_inc(lo_k, 1)

            def low_q(b):
                if b >= 2:
                    pool.wait_ge(wrote_q[b % 2], 16 * (b // 2))
                pool.wait_ge(hi_q, b + 1)
                pool.tensor_tensor(split[:, b % 2, 1, :], qf[:, b % 2, :], split[:, b % 2, 0, :].bitcast(F32),
                                   ALU.subtract).then_inc(lo_q, 1)

            def values(b):
                r = b % 2
                pool.wait_ge(s_ctxT[min(b // 2, 1)], 16)
                if b == 0:
                    pool.wait_ge(c_vzero, 1)
                if b >= 2:
                    pool.wait_ge(uz_done, 2 * (b - 1))
                src = ct_sb[:, b, :, :].rearrange("p k (g t c) -> p k g t c", t=2, c=HD)
                dst = V[:, r, :, :, :].rearrange("p k (g t) c -> p k g t c", t=2)
                pool.tensor_copy(dst[:, :, :, 0, 0:16], src[:, :, :, 0, :])
                pool.tensor_copy(dst[:, :, :, 1, 16:32], src[:, :, :, 1, :]).then_inc(v_ready, 1)

            def residual(b):
                pool.wait_ge(at_done, b + 1)
                if b == 0:
                    pool.wait_ge(c_sel, 1)
                pool.tensor_tensor(x1[:, b, :], x_sb[:, b, :], at[:, b % 2, :], ALU.add).then_inc(x1_done, 1)

            def low_w(w):
                cols = slice(w * WP, (w + 1) * WP)
                pool.wait_ge(w_hi_done, w + 1)
                pool.tensor_tensor(w_lo[:, cols], w_raw[:, w % 2, :], w_hi[:, cols].bitcast(F32),
                                   ALU.subtract).then_inc(w_lo_done, 1)

            def widen(c):
                pool.wait_ge(r_step, SELECTED * c + SELECTED)
                if c >= 1:
                    pool.wait_ge(mask_ready, 4 * c)
                for i in (2, 3):
                    pool.tensor_scalar(wide_out(i), repeated(i), LORA, None, ALU.mult).then_inc(wide_rest, 1)

            zero(Q, 0, c_zero0q)
            pool.memset(ident[:, :], 0.0).then_inc(c_ident, 1)
            pool.wait_ge(c_ident, 1)
            pool.affine_select(out=ident[:, :], in_=ident[:, :], compare_op=ALU.not_equal, fill=1.0, base=0,
                               pattern=[[-1, 128]], channel_multiplier=1).then_inc(c_ident, 1)
            low_k(0)
            low_k(1)
            pool.memset(ones[:, :, :], 0.0).then_inc(c_ones, 1)
            pool.wait_ge(c_ones, 1)
            pool.memset(ones[:, 0, 0:16], 1.0)
            pool.memset(ones[:, 1, 16:32], 1.0).then_inc(c_ones, 1)
            low_q(0)
            zero(K, 1, c_zero)
            zero(Q, 1, c_zero)
            low_k(2)
            low_q(1)
            zero(K, 2, c_zero)
            zero(Q, 2, c_zero)
            low_q(2)
            pool.memset(V[:, :, :, :, :], 0.0).then_inc(c_vzero, 1)
            values(0)
            low_k(3)
            low_q(3)
            for b in range(B):
                if 1 <= b and b + 3 < B:
                    low_k(b + 3)
                    low_q(b + 3)
                if b + 1 < B:
                    values(b + 1)
                if b >= 1:
                    residual(b - 1)
                    low_w(b - 1)
                if b == B - 2:
                    for e in range(E):
                        last = pool.memset(rev[:, :, e:e + 1], float(E - e))
                    last.then_inc(c_rev, 1)
            widen(0)
            residual(B - 1)
            low_w(WPARTS - 1)
            widen(1)

        @block.scalar
        def _(act):
            def high_k(b):
                act.wait_ge(s_ctx[group(b)], 16)
                if b >= 2:
                    act.wait_ge(wrote_k[b % 2], 16 * (b // 2))
                act.activation(split[:, b % 2, 2, :], c_sb[:, b, :], ACT.Copy).then_inc(hi_k, 1)

            def high_q(b):
                if b >= 2:
                    act.wait_ge(wrote_q[b % 2], 16 * (b // 2))
                act.wait_ge(qf_ready, b + 1)
                act.activation(split[:, b % 2, 0, :], qf[:, b % 2, :], ACT.Copy).then_inc(hi_q, 1)

            def high_w(w):
                act.wait_ge(s_w[w], 16)
                act.activation(w_hi[:, w * WP:(w + 1) * WP], w_raw[:, w % 2, :], ACT.Copy).then_inc(w_hi_done, 1)

            def max_rows(b):
                act.wait_ge(mt_ready, b + 1)
                if b >= 2:
                    act.wait_ge(rows_loaded[b % 2], 16 * (b // 2))
                act.activation(mx_rows[:, b % 2, :], MAX_BANK[0:16, 0:D], ACT.Copy).then_inc(mt_copied, 1)
                act.wait_ge(mt_copied, b + 1)
                if b >= NQ:
                    act.wait_ge(st_ready, H * (b - NQ + 1))
                act.dma_start(Q[MAXROW:MAXROW + 16, b % NQ, :, :].bitcast(F32),
                              mx_rows[:, b % 2, :].bitcast(F32).rearrange("p (a m) -> p a m", a=1).to_broadcast([16, H, D]))\
                    .then_inc(rows_loaded[b % 2], 16)

            def exp(b, i):
                n = H * b + i
                act.wait_ge(st_ready, n + 1)
                if n >= H:
                    act.wait_ge(uz_done, n // 4 - 1)
                act.activation(P[:, n % H, :, :], ST_BANK[n % 2][:, :], ACT.Exp, scale=SCALE).then_inc(exp_done, 1)

            def high_x(p):
                act.wait_ge(xT_ready, p + 1)
                act.activation(pair(xT_hi, p), turned(p), ACT.Copy).then_inc(xT_hi_done, 1)

            def copy_logits(c):
                act.wait_ge(lT_ready, c + 1)
                if c >= 1:
                    act.wait_ge(logits_ready, c)
                act.activation(lT[:, :], LOGIT_BANK[c][0:E, :], ACT.Copy).then_inc(lT_copied, 1)

            def copy_z(c, j):
                act.wait_ge(z_ready, 2 * c + j + 1)
                if c >= 1:
                    act.wait_ge(z_masked, 4 * c)
                act.activation(z_raw[:, j, :], Z_BANK[c][j][:, :], ACT.Copy).then_inc(z_copied, 1)

            def exp_logits(c):
                act.wait_ge(r_step, SELECTED * c + READ)
                if c >= 1:
                    act.wait_ge(r_step, SELECTED * c)
                act.activation(pr[:, :, :], lg[:, :, :], ACT.Exp).then_inc(r_exp, 1)

            def high_z(c, k):
                act.wait_ge(z_masked, 4 * c + k + 1)
                act.activation(z_hi[:, c, k // 2, k % 2, :], z[:, k // 2, k % 2, :], ACT.Copy).then_inc(z_hi_done, 1)

            def copy_mask(c, k):
                act.wait_ge(mask_ready, 4 * c + 2 + k + 1)
                act.activation(weight_mask[:, c, k, :], MASK_BANK[c][2 + k][:, :], ACT.Copy).then_inc(mask_copied, 1)

            def gate(n):
                m, kind = STAGES[n % NS]
                p = TAIL if m == MT - 1 else 128
                act.wait_ge(gu_ready, n + 1)
                if n >= 2:
                    act.wait_ge(hid_done, n - 1)
                for s in spans(n):
                    act.activation(silu[0:p, n % 2, s], GU_BANK[m % 2][0][0:p, s], ACT.Silu).then_inc(silu_done, 1)

            def high_h(n):
                m, kind = STAGES[n % NS]
                p = TAIL if m == MT - 1 else 128
                if n >= NH:
                    act.wait_ge(down_done, n - NH + 1)
                for o, s in enumerate(spans(n)):
                    act.wait_ge(hid_done, n + o + 1)
                    act.activation(h_hi[0:p, n % NH, s], hid[0:p, n % 3, s], ACT.Copy).then_inc(h_hi_done, 1)

            def high_a(c, o):
                n = 2 * c + o
                act.wait_ge(low_sum, n + 1)
                if c >= 1:
                    act.wait_ge(o_ready, 2 * c)
                half = slice(o * C // 2, (o + 1) * C // 2)
                act.activation(a_hi[:, half], low[:, 0, half], ACT.Copy).then_inc(a_hi_done, 1)

            high_k(0)
            high_k(1)
            high_q(0)
            act.wait_ge(c_zero0k, 1)
            act.wait_ge(s_sel[0], 16)
            act.activation(K[MAXROW:MAXROW + 16, 0, :, :], sel_sb[MAXROW:MAXROW + 16, :, :], ACT.Copy).then_inc(c_sel, 1)
            high_k(2)
            high_q(1)
            high_q(2)
            high_k(3)
            max_rows(0)
            high_q(3)
            for b in range(B):
                if b == B - 1:
                    high_x(1)
                for i in range(H):
                    exp(b, i)
                    if 1 <= b < B - 1 and i == 7:
                        high_w(b - 1)
                    if b == 0 and i == 3:
                        max_rows(1)
                    if i == 5:
                        if 1 <= b < B - 1:
                            max_rows(b + 1)
                        if b + 4 < B:
                            high_k(b + 4)
                            high_q(b + 4)
                    if b == B - 2 and i == 1:
                        high_x(0)
                    if b == B - 1 and i == 1:
                        copy_logits(0)
                    if b == B - 1 and i == 3:
                        copy_z(0, 0)
                    if b == B - 1 and i == 4:
                        exp_logits(0)
                        high_w(b - 1)
                    if b == B - 1 and i == 5:
                        copy_z(0, 1)
            high_z(0, 0)
            high_z(0, 1)
            high_w(WPARTS - 1)
            gate(0)
            copy_mask(0, 0)
            high_z(0, 2)
            high_z(0, 3)
            high_h(0)
            gate(1)
            copy_mask(0, 1)
            for n in range(2, NC * NS):
                if n == NS + 1:
                    high_a(0, 0)
                for step in (high_h, gate) if n in (NS, NC * NS - 1) else (gate, high_h):
                    step(n - (step is high_h))
                if n in (3, 5):
                    high_x(n // 2 + 1)
                if n == 6:
                    copy_logits(1)
                if n == 8:
                    exp_logits(1)
                if n in (12, 13):
                    copy_z(1, n - 12)
                if n == 15:
                    high_z(1, 0)
                    high_z(1, 1)
                if n == 16:
                    high_z(1, 2)
                    high_z(1, 3)
                if n == 17:
                    copy_mask(1, 0)
                if n == 18:
                    copy_mask(1, 1)
                if n == NS + 1:
                    high_a(0, 1)
            high_h(NC * NS - 1)
            high_a(NC - 1, 0)
            high_a(NC - 1, 1)

        @block.tensor
        def _(pe):
            def scores(b, i):
                n, q, h = H * b + i, b % NQ, ORDER[i]
                if i == 0:
                    pe.wait_ge(k_loaded[q], 16 * len(STACK_K) * (b // NQ + 1))
                    pe.wait_ge(q_loaded[q], 16 * len(STACK_Q) * (b // NQ + 1))
                if n >= 3:
                    pe.wait_ge(max_done, n - 2)
                for mh in range(2):
                    mm = pe.matmul(S_BANK[n % 3][:, mh * D:(mh + 1) * D], Q[0:96, q, h, mh * 128:(mh + 1) * 128],
                                   K[0:96, q, h, :], start=True, stop=True)
                mm.then_inc(s_ready, 1)

            def scoresT(b, i):
                n, q, h = H * b + i, b % NQ, ORDER[i]
                if i == 0:
                    if b < NQ:
                        if b == 0:
                            pe.wait_ge(c_sel, 1)
                        else:
                            pe.wait_ge(s_sel[b], 16)
                    pe.wait_ge(rows_loaded[b % 2], 16 * (b // 2 + 1))
                if n >= 2:
                    pe.wait_ge(exp_done, n - 1)
                rows = MAXROW + 16
                for nh in range(2):
                    mm = pe.matmul(ST_BANK[n % 2][:, nh * D:(nh + 1) * D], K[0:rows, q, h, nh * 128:(nh + 1) * 128],
                                   Q[0:rows, q, h, :], start=True, stop=True)
                mm.then_inc(st_ready, 1)

            def max_rows(b):
                pe.wait_ge(mx_lo, b + 1)
                if b >= 1:
                    pe.wait_ge(mt_copied, b)
                if b == B - 1:
                    pe.wait_ge(xT_hi_done, 1)
                    pe.wait_ge(xT_lo_done, 1)
                for mh in range(2):
                    mm = pe.matmul(MAX_BANK[0:16, mh * 128:(mh + 1) * 128],
                                   mx_split[:, b % 2, mh, :, :].bitcast(F32).rearrange("p a h -> p (a h)"),
                                   ident[:, :], start=True, stop=True)
                mm.then_inc(mt_ready, 1)

            def pv(b, s, halves=(0, 1)):
                if halves[0] == 0:
                    pe.wait_ge(exp_done, H * b + 4 * (s + 1))
                uz = UZ_BANK[b % 2]
                if s == 0 and halves[0] == 0:
                    pe.wait_ge(v_ready, b + 1)
                    if b >= 2:
                        pe.wait_ge(at_done, b - 1)
                for nh in halves:
                    for p in range(4):
                        pe.matmul(uz[32 * p:32 * p + 32, 0:D], V[:, b % 2, nh, 2 * p + s, :], P[:, 4 * s + p, nh, :],
                                  start=(s == 0 and nh == 0), stop=(s == 1 and nh == 1), skip_group_check=True)
                    for p in range(4):
                        mm = pe.matmul(uz[32 * p:32 * p + 32, D:2 * D], ones[:, s, :], P[:, 4 * s + p, nh, :],
                                       start=False, stop=(s == 1 and nh == 1), skip_group_check=True)
                if halves[-1] == 1:
                    mm.then_inc(uz_done, 1)

            def turn_x(p):
                pe.wait_ge(xn_done, 2 * p + 2)
                if p == 0:
                    pe.wait_ge(mt_copied, B - 1)
                if p == 1:
                    pe.wait_ge(max_done, H * B)
                if p == 2:
                    pe.wait_ge(mask_copied, 2)
                if p == 3:
                    pe.wait_ge(xT_hi_done, p)
                    pe.wait_ge(xT_lo_done, p)
                for b in (2 * p, 2 * p + 1):
                    for k in range(KD):
                        mm = pe.transpose(turned(p)[:, b % 2, k, :], xn2[:, b % 4, k * 128:(k + 1) * 128], ident[:, :])
                mm.then_inc(xT_ready, 1)

            pe.wait_ge(c_ident, 2)
            pe.wait_ge(c_ones, 2)
            xT = (xT_hi, xT_lo)

            def logits(c):
                pe.wait_ge(xT_hi_done, 2 * c + 2)
                pe.wait_ge(xT_lo_done, 2 * c + 2)
                if c == 0:
                    pe.wait_ge(w_lo_done, parts_to("wr"))
                    pe.wait_ge(mt_copied, B)
                for i, (wp, xp) in enumerate(PASSES):
                    for k in range(KD):
                        mm = pe.matmul(LOGIT_BANK[c][0:E, :], W(wp, "wr", k * E, E), xT[xp][:, k, c * C:(c + 1) * C],
                                       start=(i == 0 and k == 0), stop=(i == 2 and k == KD - 1))
                mm.then_inc(lT_ready, 1)

            def turn_logits(c):
                pe.wait_ge(lT_copied, c + 1)
                for t in range(TC):
                    mm = pe.matmul(LOGIT_BANK[c][:, t * E:(t + 1) * E], lT[:, t * 128:(t + 1) * 128], ident[0:E, 0:E],
                                   start=True, stop=True)
                mm.then_inc(logits_ready, 1)

            def z_rows(c, j):
                if c == 0:
                    pe.wait_ge(w_lo_done, parts_to("au"))
                    pe.wait_ge(max_done, H * B)
                elif j == 0:
                    pe.wait_ge(hid_done, 12)
                else:
                    pe.wait_ge(z_copied, 2 * c + 1)
                for i, (wp, xp) in enumerate(PASSES):
                    for k in range(KD):
                        mm = pe.matmul(Z_BANK[c][j][:, :], W(wp, ("ag", "au")[j], k * 128, 128),
                                       xT[xp][:, k, c * C:(c + 1) * C], start=(i == 0 and k == 0),
                                       stop=(i == 2 and k == KD - 1))
                mm.then_inc(z_ready, 1)

            def masks(c, i):
                if c == 0:
                    if i == 0:
                        pe.wait_ge(r_step, READ)
                    if i >= 2:
                        pe.wait_ge(z_masked, 2 * (i - 1))
                else:
                    if i == 0:
                        pe.wait_ge(z_copied, 2 * c + 2)
                    if i in (1, 2):
                        pe.wait_ge(z_masked, 4 * c + 2 * i)
                    if i == 3:
                        pe.wait_ge(mask_copied, 2 * c + 1)
                if i < 2:
                    pe.wait_ge(wide_first, 2 * c + i + 1)
                else:
                    pe.wait_ge(wide_rest, 2 * c + i - 1)
                for t in range(TC):
                    mm = pe.transpose(MASK_BANK[c][i][:, t * 128:(t + 1) * 128],
                                      wide[:, i, t, :, :].rearrange("p e r -> p (e r)"), ident[:, :])
                mm.then_inc(mask_ready, 1)

            def stage(c, i):
                m, kind = STAGES[i]
                n = NS * c + i
                g, u = GU_BANK[m % 2]
                if n < 2:
                    if n == 0:
                        pe.wait_ge(z_copied, 2)
                        pe.wait_ge(w_lo_done, parts_to("wu"))
                    else:
                        pe.wait_ge(exp_done, H * B)
                else:
                    pe.wait_ge(hid_done, n - 1)
                if c >= 1 and i == 1:
                    pe.wait_ge(mask_copied, 2 * c + 2)
                if n == 2:
                    pe.wait_ge(w_lo_done, parts_to("bu"))
                if i == 2:
                    pe.wait_ge(z_hi_done, 4 * c + 2)
                    pe.wait_ge(z_lo_done, 4 * c + 2)
                if i == 4:
                    pe.wait_ge(z_hi_done, 4 * c + 4)
                    pe.wait_ge(z_lo_done, 4 * c + 4)
                tail = m == MT - 1
                if kind == 0:
                    for wp, xp in PASSES:
                        for k in range(KD):
                            rhs = xT[xp][:, k, c * C:(c + 1) * C]
                            first = (wp, xp, k) == (0, 0, 0)
                            mm = pe.matmul(g[:, :], W(wp, "wg", (k * MT + m) * 128, 128), rhs,
                                           start=first, stop=False, skip_group_check=True)
                            if not tail:
                                mm = pe.matmul(u[:, :], W(wp, "wu", (k * (MT - 1) + m) * 128, 128), rhs,
                                               start=first, stop=False, skip_group_check=True)
                else:
                    for j, (name, to) in enumerate((("bg", g), ("bu", g if tail else u))):
                        for wp, zp in PASSES:
                            mm = pe.matmul(to[:, :], W(wp, name, m * 128, 128), (z_hi, z_lo)[zp][:, c, kind - 1, j, :],
                                           start=False, stop=(kind == 2), skip_group_check=True)
                mm.then_inc(gu_ready, 1)

            def down(c, i):
                m, kind = STAGES[i]
                n = NS * c + i
                s = n % NH
                pe.wait_ge(h_hi_done, n + len(spans(n)))
                pe.wait_ge(h_lo_done, n + len(spans(n)))
                if i == 0:
                    if c == 0:
                        pe.wait_ge(mask_copied, 1)
                        pe.wait_ge(at_done, B)
                        pe.wait_ge(w_lo_done, WPARTS)
                    else:
                        pe.wait_ge(y_done, 2 * c)
                if c == 0 and (m, kind) == (0, 2):
                    pe.wait_ge(r_step, SELECTED + READ)
                if c >= 1 and m == 0 and kind > 0:
                    pe.wait_ge(low_done, 3 * (c - 1) + (1, 3)[kind - 1])
                passes = [(0, h_hi), (1, h_hi)] if m == MT - 1 else [(0, h_hi), (1, h_hi), (0, h_lo)]
                for j, (wp, h) in enumerate(passes):
                    if kind == 0:
                        for t in range(TC):
                            mm = pe.matmul(O_BANK[t // 2][:, (t % 2) * D:(t % 2 + 1) * D],
                                           h[:, s, t * 128:(t + 1) * 128], W(wp, "wd", m * D, D),
                                           start=(m == 0 and j == 0 and t % 2 == 0), stop=False, skip_group_check=True)
                    else:
                        mm = pe.matmul(D_BANK[kind - 1][:, :], W(wp, "ad", m * 128, 128), h[:, s, :],
                                       start=(m == 0 and j == 0), stop=(m == MT - 1 and j == len(passes) - 1))
                mm.then_inc(down_done, 1)

            def lora_out(c, o):
                pe.wait_ge(a_hi_done, 2 * c + o + 1)
                for wp, a in ((0, a_hi), (1, a_hi), (0, a_lo)):
                    if a is a_lo:
                        pe.wait_ge(a_lo_done, 2 * c + o + 1)
                    for t in (2 * o, 2 * o + 1):
                        mm = pe.matmul(O_BANK[o][:, (t % 2) * D:(t % 2 + 1) * D], a[:, t * 128:(t + 1) * 128],
                                       W(wp, "bd", 0, D), start=False, stop=True, skip_group_check=True)
                mm.then_inc(o_ready, 1)

            for i in range(H):
                scores(0, i)
            max_rows(0)
            for i in range(H):
                scores(1, i)
            for i in range(H):
                if i == 6:
                    pv(0, 0, (0,))
                scoresT(0, i)
                if i in (1, 3, 4, 5):
                    scores(2, (1, 3, 4, 5).index(i))
                if i == 3:
                    max_rows(1)
            pv(0, 0, (1,))
            for b in range(1, B - 1):
                scoresT(b, 0)
                scores(b + 1, 4)
                scoresT(b, 1)
                scores(b + 1, 5)
                pv(b - 1, 1, (0,))
                if b == B - 2:
                    turn_x(0)
                scoresT(b, 2)
                scores(b + 1, 6)
                scoresT(b, 3)
                scores(b + 1, 7)
                pv(b - 1, 1, (1,))
                scoresT(b, 4)
                scoresT(b, 5)
                if b == B - 2:
                    pv(b, 0, (0,))
                max_rows(b + 1)
                if b != B - 2:
                    pv(b, 0, (0,))
                for i in (6, 7):
                    scoresT(b, i)
                    if b + 2 < B:
                        scores(b + 2, i - 6)
                if b + 2 < B:
                    scores(b + 2, 2)
                pv(b, 0, (1,))
                if b + 2 < B:
                    scores(b + 2, 3)
            b = B - 1
            turn_x(1)
            pv(b - 1, 1)
            for i in range(H):
                scoresT(b, i)
                if i == 1:
                    logits(0)
                if i == 3:
                    z_rows(0, 0)
                    turn_logits(0)
                if i == 5:
                    z_rows(0, 1)
                if i == 6:
                    pv(b, 0, (0,))
            masks(0, 0)
            masks(0, 1)
            pv(b, 0, (1,))
            pv(b, 1)
            for i in range(NS):
                stage(0, i)
                if i == 0:
                    masks(0, 2)
                if i == 1:
                    masks(0, 3)
                if i in (3, 5):
                    turn_x(i // 2 + 1)
                if i == 6:
                    logits(1)
                if i == 7:
                    turn_logits(1)
                if i in (12, 13):
                    z_rows(1, i - 12)
                if i == 14:
                    masks(1, 0)
                if i == 17:
                    masks(1, 2)
                if i == 8:
                    down(0, i - 1 - LAG)
                if i >= LAG and i != 7:
                    down(0, i - LAG)
                if i == 15:
                    masks(1, 1)
            for i in range(NS):
                stage(1, i)
                if i == 0:
                    masks(1, 3)
                    for j in range(NS - LAG, NS):
                        down(0, j)
                if i in (2, 3):
                    lora_out(0, i - 2)
                if i == 4:
                    down(1, 0)
                if 4 <= i < NS - 3:
                    down(1, i - LAG)
            for i in LAST_DOWNS:
                down(1, i)
            lora_out(1, 0)
            lora_out(1, 1)

        @block.vector
        def _(dve):
            def low_x(p):
                dve.wait_ge(xT_hi_done, p + 1)
                dve.tensor_tensor(pair(xT_lo, p), turned(p), pair(xT_hi, p).bitcast(F32), ALU.subtract)\
                    .then_inc(xT_lo_done, 1)

            def rsqrt_steps(which, b0, b1, done, before):
                cols = slice(b0, b1)
                v, t, y = nr_v[:, cols], nr_t[:, cols], rstd[:, which, cols]
                steps = [lambda: dve.tensor_scalar(v, mv[:, which, cols, 1], EPS, None, ALU.add),
                         lambda: dve.tensor_scalar(y.bitcast(U32), v.bitcast(U32), 1, None, ALU.logical_shift_right),
                         lambda: dve.tensor_scalar(y.bitcast(I32), y.bitcast(I32), -1, RSQRT_SEED, ALU.mult, ALU.add)]
                for _ in range(3):
                    steps += [lambda: dve.scalar_tensor_tensor(out=t, in0=y, scalar=-0.5, in1=y, op0=ALU.mult, op1=ALU.mult),
                              lambda: dve.tensor_tensor(t, t, v, ALU.mult),
                              lambda: dve.scalar_tensor_tensor(out=y, in0=t, scalar=1.5, in1=y, op0=ALU.add, op1=ALU.mult)]
                assert len(steps) == RSQRT_STEPS
                for n, step in enumerate(steps):
                    if n:
                        dve.wait_ge(done, before + n)
                    step().then_inc(done, 1)
                    yield
                dve.wait_ge(done, before + RSQRT_STEPS)
                yield

            def go_on(steps, n):
                for _ in range(n):
                    next(steps, None)

            def rsqrt(which, b0, b1, done, before):
                for _ in rsqrt_steps(which, b0, b1, done, before):
                    pass
                return before + RSQRT_STEPS

            def normalise(b):
                if b >= 4:
                    dve.wait_ge(xT_ready, (b - 4) // 2 + 1)
                dve.tensor_scalar(xn2[:, b % 4, :], x1[:, b, :], mv[:, 1, b, 0:1], rstd[:, 1, b:b + 1],
                                  ALU.subtract, ALU.mult).then_inc(xn_done, 1)

            def ln1_stats(b):
                dve.wait_ge(s_x[group(b)], 16)
                dve.bn_stats(stats[:, 0, b, :], x_sb[:, b, :]).then_inc(ln_stat, 1)
                dve.wait_ge(ln_stat, 2 * b + 1)
                dve.bn_aggr(mv[:, 0, b, :], stats[:, 0, b, :]).then_inc(ln_stat, 1)

            def q_full(b):
                if b >= 2:
                    dve.wait_ge(lo_q, b - 1)
                dve.tensor_scalar(qf[:, b % 2, :], x_sb[:, b, :], mv[:, 0, b, 0:1], rstd[:, 0, b:b + 1],
                                  ALU.subtract, ALU.mult).then_inc(qf_ready, 1)

            def maxima(b, i):
                n = H * b + i
                dve.wait_ge(s_ready, n + 1)
                if i == 0 and b >= 2:
                    dve.wait_ge(mx_lo, b - 1)
                dve.tensor_reduce(mx[:, b % 2, :, ORDER[i]], S_BANK[n % 3][:, :].rearrange("p (a n) -> p a n", a=2),
                                  AX.X, ALU.max).then_inc(max_done, 1)

            def max_split(b):
                r = b % 2
                dve.wait_ge(max_done, H * (b + 1))
                if b >= 2:
                    dve.wait_ge(mt_ready, b - 1)
                dve.tensor_copy(mx_split[:, r, :, 0, :], mx[:, r, :, :]).then_inc(mx_hi, 1)
                dve.wait_ge(mx_hi, b + 1)
                dve.tensor_tensor(mx_split[:, r, :, 1, :], mx[:, r, :, :], mx_split[:, r, :, 0, :].bitcast(F32),
                                  ALU.subtract).then_inc(mx_lo, 1)

            def norm(b):
                dve.wait_ge(uz_done, 2 * (b + 1))
                dve.reciprocal(rz[:, :], UZ_BANK[b % 2][:, D:2 * D]).then_inc(rz_done, 1)
                dve.wait_ge(rz_done, b + 1)
                if b >= 2:
                    dve.wait_ge(x1_done, b - 1)
                dve.tensor_tensor(at[:, b % 2, :], UZ_BANK[b % 2][:, 0:D], rz[:, :], ALU.mult).then_inc(at_done, 1)

            def ln2_stats(b):
                dve.wait_ge(x1_done, b + 1)
                dve.bn_stats(stats[:, 1, b, :], x1[:, b, :]).then_inc(ln2_stat, 1)
                dve.wait_ge(ln2_stat, 2 * b + 1)
                dve.bn_aggr(mv[:, 1, b, :], stats[:, 1, b, :]).then_inc(ln2_stat, 1)

            step = [0]

            def done(ins, beside=None):
                step[0] += 1
                ins.then_inc(r_step, 1)
                if beside is not None:
                    go_on(beside, 1)
                dve.wait_ge(r_step, step[0])

            def col(i):
                return mcol[:, i, :].rearrange("p (t a) -> p t a", a=1).to_broadcast([128, TC, E])

            def read_logits(c, beside=None):
                dve.wait_ge(logits_ready, c + 1)
                if c == 0:
                    dve.wait_ge(c_rev, 1)
                else:
                    dve.wait_ge(wide_rest, 2 * c)
                    dve.wait_ge(r_exp, c)
                lgt = LOGIT_BANK[c][:, 0:TC * E].rearrange("p (t e) -> p t e", e=E)
                done(dve.tensor_reduce(mcol[:, 0, :], lgt, AX.X, ALU.max), beside)
                done(dve.tensor_tensor(lg[:, :, :], lgt, col(0), ALU.subtract), beside)
                assert step[0] == SELECTED * c + READ

            def choose(c, beside=None):
                done(dve.scalar_tensor_tensor(out=tmp[:, :, :], in0=lg[:, :, :], scalar=0.0, in1=rev[:, :, :],
                                              op0=ALU.is_ge, op1=ALU.mult), beside)
                done(dve.tensor_reduce(mcol[:, 1, :], tmp[:, :, :], AX.X, ALU.max), beside)
                done(dve.tensor_tensor(sels[:, 0, :, :], rev[:, :, :], col(1), ALU.is_equal), beside)
                done(dve.scalar_tensor_tensor(out=lg2[:, :, :], in0=sels[:, 0, :, :], scalar=-3e38, in1=lg[:, :, :],
                                              op0=ALU.mult, op1=ALU.add), beside)
                done(dve.tensor_reduce(mcol[:, 2, :], lg2[:, :, :], AX.X, ALU.max), beside)
                done(dve.tensor_tensor(tmp[:, :, :], lg2[:, :, :], col(2), ALU.is_ge), beside)
                done(dve.tensor_tensor(tmp[:, :, :], tmp[:, :, :], rev[:, :, :], ALU.mult), beside)
                done(dve.tensor_reduce(mcol[:, 3, :], tmp[:, :, :], AX.X, ALU.max), beside)
                done(dve.tensor_tensor(second[:, :, :], rev[:, :, :], col(3), ALU.is_equal), beside)
                done(dve.tensor_tensor(sels[:, 1, :, :], second[:, :, :], sels[:, 0, :, :], ALU.subtract), beside)
                assert step[0] == SELECTED * c + CHOSEN
                if c >= 1:
                    dve.wait_ge(mask_ready, 4 * c)
                for i in range(2):
                    dve.tensor_scalar(wide_out(i), repeated(i), LORA, None, ALU.mult).then_inc(wide_first, 1)

            def weigh(c):
                dve.wait_ge(r_exp, c + 1)
                done(dve.tensor_reduce(mcol[:, 4, :], pr[:, :, :], AX.X, ALU.add))
                done(dve.reciprocal(mcol[:, 5, :], mcol[:, 4, :]))
                done(dve.tensor_tensor(pr[:, :, :], pr[:, :, :], col(5), ALU.mult))
                done(dve.tensor_tensor(sels[:, 2, :, :], pr[:, :, :], sels[:, 0, :, :], ALU.mult))
                done(dve.tensor_tensor(sels[:, 3, :, :], pr[:, :, :], second[:, :, :], ALU.mult))
                done(dve.tensor_copy(mcol[:, 0, :], mcol[:, 5, :]))
                assert step[0] == SELECTED * (c + 1)

            def mask_z(c, d):
                dve.wait_ge(mask_ready, 4 * c + d + 1)
                dve.wait_ge(z_copied, 2 * c + 2)
                if c >= 1:
                    dve.wait_ge(z_hi_done, 4 * c)
                    dve.wait_ge(z_lo_done, 4 * c)
                for j in range(2):
                    dve.tensor_tensor(z[:, d, j, :], z_raw[:, j, :], MASK_BANK[c][d][:, :], ALU.mult).then_inc(z_masked, 1)

            def low_z(c, d):
                for j in range(2):
                    dve.wait_ge(z_hi_done, 4 * c + 2 * d + j + 1)
                    dve.tensor_tensor(z_lo[:, c, d, j, :], z[:, d, j, :], z_hi[:, c, d, j, :].bitcast(F32),
                                      ALU.subtract).then_inc(z_lo_done, 1)

            def gate(n):
                m, kind = STAGES[n % NS]
                tail = m == MT - 1
                p = TAIL if tail else 128
                if n >= 3:
                    dve.wait_ge(h_hi_done, n - 2)
                    dve.wait_ge(h_lo_done, n - 2)
                up = GU_BANK[m % 2][0][64:128, :] if tail else GU_BANK[m % 2][1][:, :]
                for o, s in enumerate(spans(n)):
                    dve.wait_ge(silu_done, n + o + 1)
                    dve.tensor_tensor(hid[0:p, n % 3, s], silu[0:p, n % 2, s], up[:, s], ALU.mult).then_inc(hid_done, 1)

            def low_h(n):
                m, kind = STAGES[n % NS]
                tail = m == MT - 1
                p = TAIL if tail else 128
                to = h_hi[64:128, n % NH, :] if tail else h_lo[:, n % NH, :]
                for o, s in enumerate(spans(n)):
                    dve.wait_ge(h_hi_done, n + o + 1)
                    dve.wait_ge(hid_done, n + o + 1)
                    dve.tensor_tensor(to[:, s], hid[0:p, n % 3, s], h_hi[0:p, n % NH, s].bitcast(F32),
                                      ALU.subtract).then_inc(h_lo_done, 1)

            def down_rows0(c):
                dve.wait_ge(down_done, NS * c + NS - (2 if c < NC - 1 else 4))
                dve.wait_ge(mask_copied, 2 * c + 2)
                if c >= 1:
                    dve.wait_ge(a_hi_done, 2 * c)
                dve.tensor_tensor(low[:, 0, :], D_BANK[0][:, :], weight_mask[:, c, 0, :], ALU.mult).then_inc(low_done, 1)

            def down_rows1(c, o):
                dve.wait_ge(down_done, NS * (c + 1) - (c == NC - 1))
                half = slice(o * C // 2, (o + 1) * C // 2)
                dve.tensor_tensor(low[:, 1, half], D_BANK[1][:, half], weight_mask[:, c, 1, half], ALU.mult)\
                    .then_inc(low_done, 1)
                dve.wait_ge(low_done, 3 * c + o + 2)
                dve.tensor_tensor(low[:, 0, half], low[:, 0, half], low[:, 1, half], ALU.add).then_inc(low_sum, 1)

            def low_a(c, o):
                half = slice(o * C // 2, (o + 1) * C // 2)
                dve.wait_ge(a_hi_done, 2 * c + o + 1)
                if c >= 1:
                    dve.wait_ge(o_ready, 2 * c)
                dve.tensor_tensor(a_lo[:, half], low[:, 0, half], a_hi[:, half].bitcast(F32), ALU.subtract)\
                    .then_inc(a_lo_done, 1)

            def final(c, o):
                dve.wait_ge(o_ready, 2 * c + o + 1)
                if c >= 1:
                    dve.wait_ge(s_out[o], 16 * c)
                b = TC * c + 2 * o
                dve.tensor_tensor(y_sb[:, o, :], x1[:, b:b + 2, :].rearrange("p b d -> p (b d)"), O_BANK[o][:, :],
                                  ALU.add).then_inc(y_done, 1)

            dve.memset(K[:, 0, :, :].bitcast(U32), 0).then_inc(c_zero0k, 1)
            ln1_stats(0)
            dve.wait_ge(ln_stat, 2)
            at_step = rsqrt(0, 0, 1, ln_step, 0)
            q_full(0)
            for b in range(1, 4):
                ln1_stats(b)
            dve.wait_ge(ln_stat, 8)
            at_step = rsqrt(0, 1, 4, ln_step, at_step)
            q_full(1)
            q_full(2)
            for b in range(4, B):
                ln1_stats(b)
            dve.wait_ge(ln_stat, 2 * B)
            for i in range(H):
                maxima(0, i)
            max_split(0)
            q_full(3)
            ln1 = rsqrt_steps(0, 4, B, ln_step, at_step)
            go_on(ln1, 5)
            for i in range(H):
                maxima(1, i)
                go_on(ln1, 1)
            max_split(1)
            q_full(4)
            q_full(5)
            for i in range(3):
                maxima(2, i)
            for b in range(1, B - 1):
                if b == B - 3:
                    dve.wait_ge(ln2_stat, 8)
                ln2 = rsqrt_steps(1, 0, 4, ln2_step, 0) if b == B - 3 else iter(())
                for i in range(3, H):
                    maxima(b + 1, i)
                    go_on(ln2, 1)
                    if b == B - 2 and i == 5:
                        low_x(0)
                max_split(b + 1)
                go_on(ln2, 1)
                norm(b - 1)
                if b == B - 2:
                    normalise(2)
                    normalise(3)
                go_on(ln2, 1)
                if b + 2 < B:
                    for i in range(3):
                        maxima(b + 2, i)
                        go_on(ln2, 1)
                ln2_stats(b - 1)
                if b + 5 < B:
                    q_full(b + 5)
                if b == B - 3:
                    go_on(ln2, RSQRT_STEPS)
                    normalise(0)
                    normalise(1)
            low_x(1)
            norm(B - 2)
            ln2_stats(B - 2)
            dve.wait_ge(ln2_stat, 2 * (B - 1))
            ln2 = rsqrt_steps(1, 4, B - 1, ln2_step, RSQRT_STEPS)
            read_logits(0, ln2)
            choose(0, ln2)
            go_on(ln2, 1)
            weigh(0)
            for b in range(4, B - 1):
                normalise(b)
            mask_z(0, 0)
            mask_z(0, 1)
            norm(B - 1)
            low_z(0, 0)
            gate(0)
            low_z(0, 1)
            gate(1)
            low_h(0)
            ln2_stats(B - 1)
            dve.wait_ge(ln2_stat, 2 * B)
            ln2 = rsqrt_steps(1, B - 1, B, ln2_step, 2 * RSQRT_STEPS)
            for n in range(2, NC * NS):
                if n in (NS, NC * NS - 1):
                    low_h(n - 1)
                if n == 7:
                    read_logits(1)
                if n == NS + 1:
                    low_a(0, 0)
                if n == NS + 3:
                    final(0, 0)
                    final(0, 1)
                gate(n)
                if n in (14, 15):
                    mask_z(1, n - 14)
                if n in (2, 3):
                    go_on(ln2, RSQRT_STEPS // 2)
                if n not in (NS, NC * NS - 1):
                    low_h(n - 1)
                if n == 3:
                    go_on(ln2, 1)
                    normalise(B - 1)
                if n in (3, 5):
                    low_x(n // 2 + 1)
                if n == 12:
                    choose(1)
                if n == 13:
                    weigh(1)
                if n == NS:
                    down_rows0(0)
                if n in (16, 18):
                    low_z(1, n // 2 - 8)
                if n == NS:
                    down_rows1(0, 0)
                    down_rows1(0, 1)
                if n == NS + 1:
                    low_a(0, 1)
            low_h(NC * NS - 1)
            down_rows0(NC - 1)
            for o in range(2):
                down_rows1(NC - 1, o)
            for o in range(2):
                low_a(NC - 1, o)
            for o in range(2):
                final(NC - 1, o)


_OUTS = [((8, 128, 256), "float32")]


def kernel(**inputs):
    import numpy as _np
    import concourse.bacc as _bacc
    from concourse import mybir as _mybir
    from concourse.bass_utils import run_bass_kernel_spmd as _run

    a = {k: _np.ascontiguousarray(v) for k, v in inputs.items()}
    ctx_in = a["ctx_2048"]

    def tiles(m, width):
        k = m.shape[0] // 128
        o = _np.zeros((128, k, width), m.dtype)
        o[:, :, :m.shape[1]] = m.reshape(k, 128, m.shape[1]).transpose(1, 0, 2)
        return o.reshape(128, k * width)

    full, tail = (MT - 1) * 128, TAIL
    wg, wu = a["L0_ffn_Wg"].T, a["L0_ffn_Wu"].T
    wg_l = _np.concatenate([wg, wu[:, full:]], axis=1)
    wu_l = wu[:, :full]
    ag = a["L0_ffn_Ag"].reshape(E * RANK, D).T
    au = a["L0_ffn_Au"].reshape(E * RANK, D).T
    bg = a["L0_ffn_Bg"].transpose(0, 2, 1).reshape(E * RANK, F)
    bu = a["L0_ffn_Bu"].transpose(0, 2, 1).reshape(E * RANK, F)
    pad = _np.zeros((E * RANK, tail), bg.dtype)
    bg_l = _np.concatenate([bg, pad], axis=1)
    bu_l = _np.concatenate([bu[:, :full], pad, bu[:, full:]], axis=1)

    def twice_tail(m):
        return tiles(_np.concatenate([m, m[full:]], axis=0), m.shape[1])

    wd_l = twice_tail(a["L0_ffn_Wd"].T)
    ad_l = twice_tail(a["L0_ffn_Ad"].reshape(E * RANK, F).T)
    bd_l = a["L0_ffn_Bd"].transpose(0, 2, 1).reshape(E * RANK, D)
    parts = {"wg": tiles(wg_l, MT * 128), "wu": tiles(wu_l, (MT - 1) * 128), "ag": tiles(ag, 128), "au": tiles(au, 128),
             "wr": tiles(a["L0_ffn_Wr"].T, E), "bg": bg_l, "bu": bu_l, "wd": wd_l, "ad": ad_l, "bd": bd_l}
    weights = _np.concatenate([parts[name] for name, _ in PIECES], axis=1)
    sel = _np.zeros((2, H, H, D), _np.float32)
    for h in range(H):
        sel[:, h, h, :] = -1.0
    arrays = {
        "x": a["x"], "ctx_in": ctx_in, "ctxT": _np.ascontiguousarray(ctx_in.transpose(0, 2, 1)),
        "weights": _np.ascontiguousarray(weights), "sel": sel.reshape(2 * H, H, D),
    }
    nc = _bacc.Bacc("TRN2", target_bir_lowering=False, num_devices=1)
    args = [nc.dram_tensor(n, v.shape, _mybir.dt.from_np(v.dtype), kind="ExternalInput").ap() for n, v in arrays.items()]
    for i, (shape, dtype) in enumerate(_OUTS):
        args.append(nc.dram_tensor(f"out_{i}", shape, _mybir.dt.from_np(_np.dtype(dtype)), kind="ExternalOutput").ap())
    xattn_lora_ffn_kernel(nc, *args)
    r = _run(nc, [arrays], core_ids=[0])
    return r.results[0]["out_0"]
```
